# Optimizing a Trainium2 kernel written in Bass

```python
import numpy as np
import jax
import jax.numpy as jnp

def _softmax(x, axis=-1):
    return jax.nn.softmax(x, axis=axis)

def _gelu(x):
    return jax.nn.gelu(x, approximate=True)

def _silu(x):
    return jax.nn.silu(x)

def _sigmoid(x):
    return jax.nn.sigmoid(x)

def _layernorm(x, axis=-1, eps=1e-05):
    m = jnp.mean(x, axis=axis, keepdims=True)
    v = jnp.var(x, axis=axis, keepdims=True)
    return (x - m) / jnp.sqrt(v + eps)

def _scatter_add(tgt, idx, src, axis=0):
    return tgt.at[idx].add(src)

def _segment_sum(src, seg, n):
    return jax.ops.segment_sum(src, seg, n)
kernel_name = 'mk_vit_tower_d1_tok_img256_r4_21b163'

def setup_inputs(seed: int=0):
    np.random.seed(seed)
    _w = jnp.asarray

    def _rec_inputs():
        import jax
        import jax.numpy as jnp
        _rk = jax.random.key(seed)
        x = -0.000392918 + 0.999932 * jax.random.normal(jax.random.fold_in(_rk, 1), (8, 1, 128, 512), jnp.float32)
        return x
    x = _rec_inputs()

    def _L0_tok_setup():
        import jax, jax.numpy as jnp
        import numpy as np
        PATCH = 8
        EMBED = 64
        N_MELS = 128
        N_FRAMES = 512
        BATCH = 64
        NUM_PATCHES = N_MELS // PATCH * (N_FRAMES // PATCH)
        key = jax.random.key(seed)
        k1, k2, k3, k4 = jax.random.split(key, 4)
        x = jax.random.normal(k1, (BATCH, 1, N_MELS, N_FRAMES), dtype=jnp.float32)
        W = jax.random.normal(k2, (EMBED, PATCH * PATCH), dtype=jnp.float32) * (1.0 / np.sqrt(PATCH * PATCH))
        b = jax.random.normal(k3, (EMBED,), dtype=jnp.float32) * 0.01
        pos_embed = jax.random.normal(k4, (1, NUM_PATCHES, EMBED), dtype=jnp.float32) * 0.02
        return {'x': x, 'W': W, 'b': b, 'pos_embed': pos_embed}
    _L0_tok_all = _L0_tok_setup()
    _L0_tok_in = {k: v for k, v in _L0_tok_all.items() if k in ('W', 'b', 'pos_embed')}
    del _L0_tok_all

    def _L0_attn_setup():
        import jax, jax.numpy as jnp
        import numpy as np
        NUM_HEADS = 8

        def _to_heads(y, R, C, H, hd):
            y = y.reshape(R, C, H, hd).transpose(0, 2, 1, 3)
            y = jnp.transpose(y, (2, 1, 0, 3)).reshape(1, H, C, R * hd)
            return y

        def _reference_tuple_inner(x, Wq, bq, Wk, bk, Wv, bv):
            R, C, E = x.shape
            H = NUM_HEADS
            hd = E // H
            q = _to_heads(x @ Wq.T + bq, R, C, H, hd)
            k = _to_heads(x @ Wk.T + bk, R, C, H, hd)
            v = _to_heads(x @ Wv.T + bv, R, C, H, hd)
            d = q.shape[-1]
            q = jax.nn.softmax(q, axis=-1)
            k = jax.nn.softmax(k, axis=-2)
            q = q * jnp.asarray(float(d) ** 0.5, dtype=q.dtype)
            attn_weights = jnp.einsum('bhnd,bhmd->bhnm', q, k).sum(0)
            context = jnp.einsum('bhnd,bhne->bhde', k, v)
            out = jnp.einsum('bhnd,bhde->hbne', q, context)
            out = out.reshape(H, C, R, hd)
            out = jnp.transpose(out, (2, 1, 0, 3)).reshape(R, C, E)
            return (out, attn_weights)
        key = jax.random.key(seed)
        ks = jax.random.split(key, 7)
        R, C, E = (16, 512, 64)
        x = jax.random.normal(ks[0], (R, C, E), dtype=jnp.float32)
        s = 0.02
        Wq = jax.random.normal(ks[1], (E, E), dtype=jnp.float32) * s
        bq = jax.random.normal(ks[2], (E,), dtype=jnp.float32) * s
        Wk = jax.random.normal(ks[3], (E, E), dtype=jnp.float32) * s
        bk = jax.random.normal(ks[4], (E,), dtype=jnp.float32) * s
        Wv = jax.random.normal(ks[5], (E, E), dtype=jnp.float32) * s
        bv = jax.random.normal(ks[6], (E,), dtype=jnp.float32) * s
        return {'x': x, 'Wq': Wq, 'bq': bq, 'Wk': Wk, 'bk': bk, 'Wv': Wv, 'bv': bv}
    _L0_attn_all = _L0_attn_setup()
    _L0_attn_in = {k: v for k, v in _L0_attn_all.items() if k in ('Wq', 'bq', 'Wk', 'bk', 'Wv', 'bv')}
    del _L0_attn_all

    def _L0_ffn_setup():
        import jax, jax.numpy as jnp
        import numpy as np
        B, S, D, E, H, K = (4, 1024, 64, 8, 128, 2)
        key = jax.random.key(seed)
        ks = jax.random.split(key, 6)
        x = jax.random.normal(ks[0], (B, S, D), jnp.float32)
        Wg = jax.random.normal(ks[1], (D, E), jnp.float32) * 0.02
        bg = jnp.zeros((E,), jnp.float32)
        W1 = jax.random.normal(ks[2], (E, D, H), jnp.float32) * 0.02
        b1 = jnp.zeros((E, H), jnp.float32)
        W2 = jax.random.normal(ks[3], (E, H, D), jnp.float32) * 0.02
        b2 = jnp.zeros((E, D), jnp.float32)
        return {'x': x, 'Wg': Wg, 'bg': bg, 'W1': W1, 'b1': b1, 'W2': W2, 'b2': b2}
    _L0_ffn_all = _L0_ffn_setup()
    _L0_ffn_in = {k: v for k, v in _L0_ffn_all.items() if k in ('Wg', 'bg', 'W1', 'b1', 'W2', 'b2')}
    del _L0_ffn_all
    return {'x': x, 'L0_tok_W': _L0_tok_in['W'], 'L0_tok_b': _L0_tok_in['b'], 'L0_tok_pos_embed': _L0_tok_in['pos_embed'], 'L0_attn_Wq': _L0_attn_in['Wq'], 'L0_attn_bq': _L0_attn_in['bq'], 'L0_attn_Wk': _L0_attn_in['Wk'], 'L0_attn_bk': _L0_attn_in['bk'], 'L0_attn_Wv': _L0_attn_in['Wv'], 'L0_attn_bv': _L0_attn_in['bv'], 'L0_ffn_Wg': _L0_ffn_in['Wg'], 'L0_ffn_bg': _L0_ffn_in['bg'], 'L0_ffn_W1': _L0_ffn_in['W1'], 'L0_ffn_b1': _L0_ffn_in['b1'], 'L0_ffn_W2': _L0_ffn_in['W2'], 'L0_ffn_b2': _L0_ffn_in['b2']}

def reference(x, L0_tok_W, L0_tok_b, L0_tok_pos_embed, L0_attn_Wq, L0_attn_bq, L0_attn_Wk, L0_attn_bk, L0_attn_Wv, L0_attn_bv, L0_ffn_Wg, L0_ffn_bg, L0_ffn_W1, L0_ffn_b1, L0_ffn_W2, L0_ffn_b2):
    import jax
    import jax.numpy as jnp

    def _L0_tok_ref(x, W, b, pos_embed):
        import jax, jax.numpy as jnp
        import numpy as np
        PATCH = 8
        EMBED = 64
        N_MELS = 128
        N_FRAMES = 512
        BATCH = 64
        NUM_PATCHES = N_MELS // PATCH * (N_FRAMES // PATCH)
        B = x.shape[0]
        mp, fp = (N_MELS // PATCH, N_FRAMES // PATCH)
        xs = x[:, 0]
        patches = xs.reshape(B, mp, PATCH, fp, PATCH).transpose(0, 1, 3, 2, 4).reshape(B, mp * fp, PATCH * PATCH)
        emb = jnp.einsum('bnk,ek->bne', patches, W) + b
        return emb + pos_embed

    def _L0_attn_ref(x, Wq, bq, Wk, bk, Wv, bv):
        import jax, jax.numpy as jnp
        import numpy as np
        NUM_HEADS = 8

        def _to_heads(y, R, C, H, hd):
            y = y.reshape(R, C, H, hd).transpose(0, 2, 1, 3)
            y = jnp.transpose(y, (2, 1, 0, 3)).reshape(1, H, C, R * hd)
            return y

        def _reference_tuple_inner(x, Wq, bq, Wk, bk, Wv, bv):
            R, C, E = x.shape
            H = NUM_HEADS
            hd = E // H
            q = _to_heads(x @ Wq.T + bq, R, C, H, hd)
            k = _to_heads(x @ Wk.T + bk, R, C, H, hd)
            v = _to_heads(x @ Wv.T + bv, R, C, H, hd)
            d = q.shape[-1]
            q = jax.nn.softmax(q, axis=-1)
            k = jax.nn.softmax(k, axis=-2)
            q = q * jnp.asarray(float(d) ** 0.5, dtype=q.dtype)
            attn_weights = jnp.einsum('bhnd,bhmd->bhnm', q, k).sum(0)
            context = jnp.einsum('bhnd,bhne->bhde', k, v)
            out = jnp.einsum('bhnd,bhde->hbne', q, context)
            out = out.reshape(H, C, R, hd)
            out = jnp.transpose(out, (2, 1, 0, 3)).reshape(R, C, E)
            return (out, attn_weights)
        return _reference_tuple_inner(x, Wq, bq, Wk, bk, Wv, bv)[0]

    def _L0_ffn_ref(x, Wg, bg, W1, b1, W2, b2):
        import jax, jax.numpy as jnp
        import numpy as np
        B, S, D, E, H, K = (4, 1024, 64, 8, 128, 2)
        Bv, Sv, Dv = x.shape
        gate_scores = x @ Wg + bg
        _, idx = jax.lax.top_k(gate_scores, K)
        mask = jax.nn.one_hot(idx, E, dtype=x.dtype).sum(axis=-2)
        xf = x.reshape(-1, Dv)
        mf = mask.reshape(-1, E)
        h = jax.nn.gelu(jnp.einsum('td,edh->teh', xf, W1) + b1[None], approximate=False)
        y = jnp.einsum('teh,ehd->ted', h, W2) + b2[None]
        out = jnp.einsum('ted,te->td', y, mf)
        return out.reshape(Bv, Sv, Dv)
    h = _L0_tok_ref(x, L0_tok_W, L0_tok_b, L0_tok_pos_embed)
    h = h + _L0_attn_ref(_layernorm(h, axis=-1), L0_attn_Wq, L0_attn_bq, L0_attn_Wk, L0_attn_bk, L0_attn_Wv, L0_attn_bv)
    h = h + _L0_ffn_ref(_layernorm(h, axis=-1), L0_ffn_Wg, L0_ffn_bg, L0_ffn_W1, L0_ffn_b1, L0_ffn_W2, L0_ffn_b2)
    return h

_drawn_inputs = setup_inputs


def setup_inputs(seed=0):
    import zlib

    import numpy as np

    out = dict(_drawn_inputs(seed))
    spreads = {'L0_ffn_bg': (0.0, 0.1), 'L0_ffn_b1': (0.0, 0.539), 'L0_ffn_b2': (0.0, 0.1)}
    factors = {'L0_tok_b': 3.119,
     'L0_attn_Wq': 8.0,
     'L0_attn_bq': 53.809,
     'L0_attn_Wk': 8.0,
     'L0_attn_bk': 42.011}
    for name, (base, spread) in spreads.items():
        noise = np.random.default_rng([zlib.crc32(name.encode()), seed]).standard_normal(out[name].shape)
        drawn = base * np.exp(spread * noise) if base else spread * noise
        out[name] = jnp.asarray(drawn.astype(out[name].dtype))
    for name, factor in factors.items():
        out[name] = (out[name] * factor).astype(out[name].dtype)
    return out
```

```python
from contextlib import ExitStack

import concourse.bass as bass
from concourse import mybir

F32 = mybir.dt.float32
F32R = mybir.dt.float32r
ALU = mybir.AluOpType
ACT = mybir.ActivationFunctionType
AX = mybir.AxisListType

P = 128
R = 8
C = 1024
E = 64
NH = 8
HD = E // NH
PATCH = 8
ROW = R * E
NX = 8
HID = 128
NG = 16
GT = 4
GW = GT * E
NM = 18
KM = E + NM
EPS = 1e-5
BIG = float(2 ** 100)
FAR = -3.0e38


class Chain:

    def __init__(self, eng, sem):
        self.eng, self.sem, self.value, self.links = eng, sem, 0, 0

    def link(self, ins):
        self.value = self.value + 1
        self.links += 1
        ins.then_inc(self.sem, 1)
        self.eng.wait_ge(self.sem, self.value)


def bass_vit_layer_kernel(nc, x, tok_w, tok_b, pos, wq, bq, wk, bk, wv, bv, wg, bg, w1, b1, w2, b2,
                          c_ident, c_rows, c_coef, c_prio, out):
    h_dram = nc.dram_tensor("residual_by_patch", (C, ROW), F32, kind="Internal").ap()

    with ExitStack() as ctx:
        def sb(name, shape, dt=F32):
            return ctx.enter_context(nc.sbuf_tensor(name, shape, dt))

        def sem(name):
            return ctx.enter_context(nc.semaphore(name))

        ident = sb("ident", [P, P])
        w_rows = sb("w_rows", [E, 4, 2, E])
        w_bd = sb("w_bd", [P, 4, P])
        biases = sb("biases", [P, 4, E])
        ones_row = sb("ones_row", [E, P])
        ones_bd = sb("ones_bd", [P, 2])
        minus_half = sb("minus_half", [P, 8])
        w1_raw = sb("w1_raw", [P, NX, HID])
        w1_hh = sb("w1_hh", [P, NX, HID], F32R)
        aug_raw = sb("aug_raw", [KM, NX * HID])
        aug_round = sb("aug_round", [KM, NX * HID], F32R)
        aug_part = sb("aug_part", [KM, NX * HID])
        w_aug = sb("w_aug", [KM, NX * HID], F32R)
        coef = sb("coef", [KM, 2])
        b2_raw = sb("b2_raw", [KM, 2 * E])
        b2_round = sb("b2_round", [KM, 2 * E], F32R)
        b2_aug = sb("b2_aug", [KM, 2 * E], F32R)
        w2_sb = sb("w2_sb", [HID, NX, E])
        wg_sb = sb("wg_sb", [E, NX])
        bg_sb = sb("bg_sb", [P, NX])
        prio = sb("prio", [P, NX])

        x_sb = sb("x_sb", [P, 2, PATCH, 32, PATCH])
        x_pt = sb("x_pt", [P, 32, 2, PATCH, PATCH])
        pt = sb("pt", [P, 4, NH, P])
        posb = sb("posb", [P, NH, E])
        h_sb = sb("h_sb", [P, NH, ROW])
        xc = sb("xc", [P, NH, ROW])
        sq = x_sb[:].rearrange("p q k f w -> p (q k f w)").rearrange("p (g f) -> p g f", g=NH)
        s1 = sb("s1", [P, NH, R])
        s2 = sb("s2", [P, NH, R])
        var = sb("var", [P, NH, R])
        rstd = sb("rstd", [P, NH, R])

        xn = sb("xn", [P, 2, ROW])
        xnt = sb("xnt", [P, 2, 4, P])
        kb = sb("kb", [P, 2, R, NH, HD])
        qb = sb("qb", [P, 2, R, NH, HD])
        eq = sb("eq", [P, 2, NH, E])
        ek = sb("ek", [P, 2, NH, E])
        vb = sb("vb", [P, 2, NH, E + 1])
        kmax_h = sb("kmax_h", [P, 2, E])
        kmax = sb("kmax", [E, 2])
        kdiag = sb("kdiag", [E, E])
        qmax = sb("qmax", [P, 2, NH])
        qinv = sb("qinv", [P, 2, NH])
        kinv = sb("kinv", [P, 2])
        ctx_bd = sb("ctx_bd", [P, 2, P])
        eqt = sb("eqt", [P, 2, 4, P])
        att = sb("att", [P, 2, NH, E])
        h2 = sb("h2", [P, NH, R, E])

        xc2 = sb("xc2", [P, 2, GT, E])
        sq2 = sb("sq2", [P, 2, GT, E])
        s1b = sb("s1b", [P, 2, GT])
        s2b = sb("s2b", [P, 2, GT])
        var2 = sb("var2", [P, 2, GT])
        rstd2 = sb("rstd2", [P, 2, GT])
        xn2 = sb("xn2", [P, 2, GT, E])
        xt = sb("xt", [E, 2, 512])
        xhl = [sb(f"xhl{n}", [P, 512], F32R) for n in range(2)]
        xm = [sb(f"xm{n}", [KM, 512], F32R) for n in range(2)]
        score = sb("score", [P, GT, NX])
        score2 = sb("score2", [P, GT, NX])
        hit = sb("hit", [P, GT, NX])
        pick = sb("pick", [P, 2, GT, NX])
        best = sb("best", [P, 4, GT])
        mask = sb("mask", [P, 2, GT, NM])
        hid = sb("hid", [HID, 2, 2, 512])
        ys = sb("ys", [P, 2, 512])
        osum = sb("osum", [P, 2, GT, E])
        o_sb = xc[:].rearrange("p g (t f) -> p (g t) f", t=2)

        ps = ctx.enter_context(nc.psum_tensor("ps", [P, 8, 512], F32))

        ld_ident, ld_w, ld_bias, x_ready = sem("ld_ident"), sem("ld_w"), sem("ld_bias"), sem("x_ready")
        ld_x = [sem(f"ld_x{n}") for n in range(4)]
        ld_ffn = sem("ld_ffn")
        res_out, res_in = sem("res_out"), sem("res_in")
        stored = [sem("stored_even"), sem("stored_odd")]
        zeroed, wt_ps, wbd_ready, posb_ready = sem("zeroed"), sem("wt_ps"), sem("wbd_ready"), sem("posb_ready")
        pt_ps, pt_act, pt_dve = sem("pt_ps"), sem("pt_act"), sem("pt_dve")
        emb_ps, h_ready, xc_ready, sq_ready = sem("emb_ps"), sem("h_ready"), sem("xc_ready"), sem("sq_ready")
        var_ready, rstd_ready = sem("var_ready"), sem("rstd_ready")
        rounded, ffn_w_ready = sem("rounded"), sem("ffn_w_ready")
        xn_ready, xnt_ps, xnt_ready = sem("xn_ready"), sem("xnt_ps"), sem("xnt_ready")
        k_ps, q_ps, v_ps = sem("k_ps"), sem("q_ps"), sem("v_ps")
        kb_ready, kmaxh_ready, kmaxt_ps, kdiag_ready = sem("kb_ready"), sem("kmaxh_ready"), sem("kmaxt_ps"), sem("kdiag_ready")
        kbc_ps, ksub_done, ek_ready = sem("kbc_ps"), sem("ksub_done"), sem("ek_ready")
        qb_ready, qmax_ready, qsub_done, eq_ready = sem("qb_ready"), sem("qmax_ready"), sem("qsub_done"), sem("eq_ready")
        eqt_ps, eqt_ready, vb_ready = sem("eqt_ps"), sem("eqt_ready"), sem("vb_ready")
        ctx_ps, ctx_ready, att_ps, qinv_ready = sem("ctx_ps"), sem("ctx_ready"), sem("att_ps"), sem("qinv_ready")
        att_ready, h2_ready = sem("att_ready"), sem("h2_ready")
        xc2_ready, sq2_ready, var2_ready, rstd2_ready = sem("xc2_ready"), sem("sq2_ready"), sem("var2_ready"), sem("rstd2_ready")
        xn2_ready, xt_ps, xt_ready, xmx_ready = sem("xn2_ready"), sem("xt_ps"), sem("xt_ready"), sem("xmx_ready")
        xhl_ready, gate_ps, score_read, mask_ready = sem("xhl_ready"), sem("gate_ps"), sem("score_read"), sem("mask_ready")
        mask_ps, xmm_ready = sem("mask_ps"), sem("xmm_ready")
        up_ps, hid_ready, down_ps = sem("up_ps"), sem("hid_ready"), sem("down_ps")
        ys_ready, yt_ps, out_ready = sem("ys_ready"), sem("yt_ps"), sem("out_ready")
        dve_chain, pool_chain = sem("dve_chain"), sem("pool_chain")

        block = ctx.enter_context(nc.Block())

        B_XNT, B_K, B_Q, B_V, B_KMAX, B_CTX, B_EQT, B_ATT = range(8)
        QS = 80
        B_DOWN, B_T, B_GATE, B_YT = 4, 5, 6, 7

        def load_x(eng, fh):
            images = x.rearrange("(q b) o (m p) c -> q (b o m) p c", q=2, p=PATCH)
            for q in range(2):
                eng.dma_start(x_sb[fh * 64:(fh + 1) * 64, q].rearrange("m p f w -> m p (f w)"),
                              images[q, :, :, fh * 256:(fh + 1) * 256]).then_inc(ld_x[2 * fh + q], 16)

        def regroup_x(eng, copy, fh):
            at = slice(fh * 64, (fh + 1) * 64)
            for q in range(2):
                eng.wait_ge(ld_x[2 * fh + q], 16)
                copy(x_pt[at, :, q].rearrange("m f p w -> m p f w"), x_sb[at, q]).then_inc(x_ready, 1)

        def patches_out(t):
            return (pt[:].rearrange("k b g (m a f) -> k f a (b g m)", m=2, a=2)[:, 4 * t:4 * t + 4],
                    ps[:, t, :].rearrange("k (f a c) -> k f a c", f=4, a=2))

        @block.sync
        def _(sp):
            sp.dma_start(ident[:], c_ident).then_inc(ld_ident, 16)
            load_x(sp, 0)
            for n, b in enumerate((tok_b, bq, bk, bv)):
                sp.dma_start(biases[:, n, :], b.partition_broadcast(P)).then_inc(ld_bias, 16)
            sp.dma_start(posb[:], pos[0].rearrange("(g c) e -> c g e", g=NH)).then_inc(ld_bias, 16)
            w1_in = w1.rearrange("x d h -> d x h")
            for half in range(2):
                sp.dma_start(w1_raw[half * E:(half + 1) * E], w1_in).then_inc(ld_ffn, 16)
            sp.dma_start(aug_raw[0:E].rearrange("d (x h) -> d x h", x=NX), w1_in).then_inc(ld_ffn, 16)
            sp.dma_start(aug_raw[E:E + 16], c_rows).then_inc(ld_ffn, 16)
            for n in range(2):
                sp.dma_start(aug_raw[E + 16 + n:E + 17 + n],
                             b1.rearrange("(a x) h -> a (x h)", a=1)).then_inc(ld_ffn, 16)
            sp.wait_ge(zeroed, 1)
            for n in range(2):
                sp.dma_start(b2_raw[E + 8:E + 16, n * E:(n + 1) * E], b2).then_inc(ld_ffn, 16)
            sp.dma_start(coef[:], c_coef).then_inc(ld_ffn, 16)
            sp.dma_start(w2_sb[:], w2.rearrange("x h d -> h x d")).then_inc(ld_ffn, 16)
            sp.dma_start(wg_sb[:], wg).then_inc(ld_ffn, 16)
            sp.dma_start(bg_sb[:], bg.partition_broadcast(P)).then_inc(ld_ffn, 16)
            sp.dma_start(prio[:], c_prio).then_inc(ld_ffn, 16)
            res_rows = h_dram.rearrange("(g c) f -> g c f", g=NH)
            with sp.Fori(0, NH) as g:
                sp.wait_ge(h_ready, g + 1)
                sp.dma_start(res_rows[g], h_sb[:, g, :]).then_inc(res_out, 16)
            sp.wait_ge(res_out, 16 * NH)
            sp.dma_start(h2[:].rearrange("a j r e -> a (j r e)"),
                         h_dram.rearrange("(a j) f -> a (j f)", j=8)).then_inc(res_in, 16)
            out_v = out.rearrange("r (a j) e -> j a r e", j=8)
            with sp.Fori(0, NG // 2) as j:
                for half in range(2):
                    sp.wait_ge(out_ready, 2 * j + half + 1)
                    sp.dma_start(out_v[j, :, GT * half:GT * (half + 1), :],
                                 o_sb[:, 2 * j + half, :].rearrange("a (r e) -> a r e", r=GT)).then_inc(stored[half], 16)
            for half in range(2):
                sp.wait_ge(stored[half], 16 * (NG // 2))

        @block.gpsimd
        def _(pool):
            nc.gpsimd.memset(b2_raw[:], 0.0).then_inc(zeroed, 1)
            nc.gpsimd.memset(w_bd[:], 0.0).then_inc(zeroed, 1)
            nc.gpsimd.memset(ctx_bd[:], 0.0).then_inc(zeroed, 1)
            nc.gpsimd.memset(ones_bd[:], 0.0).then_inc(zeroed, 1)
            nc.gpsimd.memset(ones_row[:], 1.0).then_inc(zeroed, 1)
            nc.gpsimd.memset(vb[:], 1.0).then_inc(zeroed, 1)
            nc.gpsimd.memset(mask[:], 1.0).then_inc(zeroed, 1)
            nc.gpsimd.memset(minus_half[:], -0.5).then_inc(zeroed, 1)
            pool.wait_ge(zeroed, 8)
            nc.gpsimd.memset(ones_bd[0:E, 0:1], 1.0).then_inc(zeroed, 1)
            pool.wait_ge(zeroed, 9)
            nc.gpsimd.memset(ones_bd[E:P, 1:2], 1.0).then_inc(zeroed, 1)
            pool.wait_ge(zeroed, 10)
            pool.wait_ge(ld_bias, 16 * 5)
            nc.gpsimd.tensor_tensor(posb[:], posb[:], biases[:, 0, :].unsqueeze(1).to_broadcast([P, NH, E]),
                                    ALU.add).then_inc(posb_ready, 1)
            with pool.Fori(0, NH) as g:
                pool.wait_ge(var_ready, g + 1)
                nc.gpsimd.tensor_tensor(rstd[:, g, :], var[:, g, :], minus_half[:], ALU.pow).then_inc(rstd_ready, 1)

            def normalise(g, p):
                nc.gpsimd.tensor_tensor(xn[:, p].rearrange("c (r e) -> c r e", r=R),
                                        xc[:, g, :].rearrange("c (r e) -> c r e", r=R),
                                        rstd[:, g, :].unsqueeze(2).to_broadcast([P, R, E]), ALU.mult)\
                    .then_inc(xn_ready, 1)

            def queries_minus_max(s, p):
                pool.wait_ge(qmax_ready, s + 1)
                nc.gpsimd.tensor_tensor(qb[:, p], qb[:, p],
                                        qmax[:, p].unsqueeze(1).unsqueeze(3).to_broadcast([P, R, NH, HD]),
                                        ALU.subtract).then_inc(qsub_done, 1)

            def add_attention(g, p):
                pool.wait_ge(att_ready, g + 1)
                dst = h2[:].rearrange("a j r e -> a (j r) e")[:, :, bass.ds(g * HD, HD)]
                nc.gpsimd.tensor_tensor(dst, dst, att[:, p].rearrange("a j (r d) -> a (j r) d", d=HD),
                                        ALU.add).then_inc(h2_ready, 1)

            def step(s, p):
                queries_minus_max(s, p)
                pool.wait_ge(xnt_ps, s)
                normalise(s + 1, 1 - p)
                add_attention(s - 1, 1 - p)

            pool.wait_ge(rstd_ready, NH)
            normalise(0, 0)
            queries_minus_max(0, 0)
            normalise(1, 1)
            pool.wait_ge(res_in, 16)
            with pool.Fori(0, 3) as i:
                step(2 * i + 1, 1)
                step(2 * i + 2, 0)
            queries_minus_max(7, 1)
            add_attention(6, 0)
            add_attention(7, 1)

            def norm2(u, p):
                pool.wait_ge(var2_ready, u + 1)
                nc.gpsimd.tensor_tensor(rstd2[:, p], var2[:, p], minus_half[:, 0:GT], ALU.pow)\
                    .then_inc(rstd2_ready, 1)
                pool.wait_ge(rstd2_ready, u + 1)
                nc.gpsimd.tensor_tensor(xn2[:, p], xc2[:, p],
                                        rstd2[:, p].unsqueeze(2).to_broadcast([P, GT, E]), ALU.mult)\
                    .then_inc(xn2_ready, 1)

            norm2(0, 0)
            norm2(1, 1)
            with pool.Fori(0, NG // 2 - 1) as i:
                for n in range(2):
                    u = 2 * i + 2 + n
                    pool.wait_ge(xt_ps, u - 1)
                    norm2(u, n)

        @block.scalar
        def _(act):
            load_x(act, 1)
            for n, w in enumerate((tok_w, wq, wk, wv)):
                for twice in range(2):
                    act.dma_start(w_rows[:, n, twice, :], w).then_inc(ld_w, 16)
            regroup_x(act, nc.scalar.copy, 1)
            for t in range(1, 8, 2):
                act.wait_ge(pt_ps, t + 1)
                dst, src = patches_out(t)
                nc.scalar.activation(dst, src, ACT.Copy).then_inc(pt_act, 1)
            with act.Fori(0, NH) as g:
                act.wait_ge(xc_ready, g + 1)
                nc.scalar.activation(sq[:, g, :], xc[:, g, :], ACT.Square).then_inc(sq_ready, 1)
            act.wait_ge(ld_ffn, 16 * 13)
            nc.scalar.activation(w1_hh[:], w1_raw[:], ACT.Copy).then_inc(rounded, 1)
            nc.scalar.activation(aug_round[:], aug_raw[:], ACT.Copy).then_inc(rounded, 1)
            nc.scalar.activation(aug_part[:], aug_raw[:], ACT.Copy, scale=coef[:, 0:1]).then_inc(rounded, 1)
            nc.scalar.activation(b2_round[:], b2_raw[:], ACT.Copy).then_inc(rounded, 1)

            def xnt_copy(g, p):
                act.wait_ge(xnt_ps, g + 1)
                nc.scalar.activation(xnt[:, p].rearrange("k b c -> k (b c)"), ps[:, B_XNT, :], ACT.Copy)\
                    .then_inc(xnt_ready, 1)

            def by_row(t, p):
                return t[:, p].rearrange("c h (r d) -> c r h d", r=R)

            def softmaxes(s, p):
                act.wait_ge(qsub_done, s + 1)
                nc.scalar.activation(by_row(eq, p), qb[:, p], ACT.Exp).then_inc(eq_ready, 1)
                act.wait_ge(ksub_done, s + 1)
                nc.scalar.activation(by_row(ek, p), kb[:, p], ACT.Exp).then_inc(ek_ready, 1)

            def eqt_copy(s, p):
                act.wait_ge(eqt_ps, s + 1)
                nc.scalar.activation(eqt[:, p].rearrange("k b c -> k (b c)"), ps[:, B_EQT, :], ACT.Copy)\
                    .then_inc(eqt_ready, 1)

            def step(s, p):
                softmaxes(s, p)
                eqt_copy(s, p)
                act.wait_ge(v_ps, s)
                xnt_copy(s + 1, 1 - p)

            xnt_copy(0, 0)
            softmaxes(0, 0)
            eqt_copy(0, 0)
            xnt_copy(1, 1)
            with act.Fori(0, 3) as i:
                step(2 * i + 1, 1)
                step(2 * i + 2, 0)
            softmaxes(7, 1)
            eqt_copy(7, 1)

            def squares(u, p):
                act.wait_ge(xc2_ready, u + 1)
                nc.scalar.activation(sq2[:, p], xc2[:, p], ACT.Square).then_inc(sq2_ready, 1)

            def tokens_copy(u, p):
                act.wait_ge(xt_ps, u + 1)
                nc.scalar.activation(xt[:, p], ps[0:E, B_T, :], ACT.Copy).then_inc(xt_ready, 1)

            def tokens_round(u, p):
                nc.scalar.activation(xm[p][0:E], ps[0:E, B_T, :], ACT.Copy).then_inc(xmx_ready, 1)

            def mask_copy(u, p):
                act.wait_ge(mask_ps, u + 1)
                nc.scalar.activation(xm[p][E:KM], ps[0:NM, B_GATE, :], ACT.Copy).then_inc(xmm_ready, 1)

            def gelu(u, pair, wait_hid=True):
                act.wait_ge(up_ps, 4 * u + pair + 1)
                if wait_hid:
                    act.wait_ge(down_ps, 4 * u + pair - 1)
                at = 2 * (pair % 2)
                nc.scalar.activation(hid[:, pair % 2], ps[:, at:at + 2, :], ACT.Gelu).then_inc(hid_ready, 1)

            def group(u, p, first=False, prep=True, norm=True):
                if prep:
                    if not first:
                        act.wait_ge(up_ps, 4 * u)
                    tokens_copy(u + 1, 1 - p)
                gelu(u, 0, not first)
                if prep:
                    tokens_round(u + 1, 1 - p)
                gelu(u, 1, not first)
                if norm:
                    squares(u + 2, p)
                gelu(u, 2)
                if prep:
                    mask_copy(u + 1, 1 - p)
                gelu(u, 3)

            squares(0, 0)
            squares(1, 1)
            tokens_copy(0, 0)
            tokens_round(0, 0)
            mask_copy(0, 0)
            group(0, 0, first=True)
            with act.Fori(0, 6) as i:
                group(2 * i + 1, 1)
                group(2 * i + 2, 0)
            group(13, 1)
            group(14, 0, norm=False)
            group(15, 1, prep=False, norm=False)

        @block.vector
        def _(dve):
            chain = Chain(dve, dve_chain)
            regroup_x(dve, nc.vector.tensor_copy, 0)
            dve.wait_ge(zeroed, 10)
            dve.wait_ge(wt_ps, 1)
            wt = ps[:, 7, 0:4 * E].rearrange("k (w e) -> k w e", w=4)
            nc.vector.tensor_copy(w_bd[0:E, :, 0:E], wt[0:E]).then_inc(wbd_ready, 1)
            nc.vector.tensor_copy(w_bd[E:P, :, E:P], wt[E:P]).then_inc(wbd_ready, 1)
            for t in range(0, 8, 2):
                dve.wait_ge(pt_ps, t + 1)
                dst, src = patches_out(t)
                nc.vector.tensor_copy(dst, src).then_inc(pt_dve, 1)

            def rows(t, g):
                return t[:, g, :].rearrange("c (r e) -> c r e", r=R)

            def embed(g):
                dve.wait_ge(emb_ps, g + 1)
                nc.vector.tensor_tensor(rows(h_sb, g), rows(ps, g),
                                        posb[:, g, :].unsqueeze(1).to_broadcast([P, R, E]), ALU.add)\
                    .then_inc(h_ready, 1)
                dve.wait_ge(h_ready, g + 1)
                chain.link(nc.vector.tensor_reduce(s1[:, g, :], rows(h_sb, g), AX.X, ALU.add))
                nc.vector.scalar_tensor_tensor(out=rows(xc, g), in0=s1[:, g, :].unsqueeze(2).to_broadcast([P, R, E]),
                                               scalar=-1.0 / E, in1=rows(h_sb, g), op0=ALU.mult, op1=ALU.add)\
                    .then_inc(xc_ready, 1)

            def variance(g):
                dve.wait_ge(sq_ready, g + 1)
                chain.link(nc.vector.tensor_reduce(s2[:, g, :], rows(sq, g), AX.X, ALU.add))
                nc.vector.tensor_scalar(var[:, g, :], s2[:, g, :], 1.0 / E, EPS, ALU.mult, ALU.add)\
                    .then_inc(var_ready, 1)

            dve.wait_ge(posb_ready, 1)
            embed(0)
            base, per = chain.value, 2
            with dve.Fori(0, NH - 1) as i:
                chain.value = base + i * per
                embed(i + 1)
                variance(i)
            chain.value = base + (NH - 1) * per
            variance(NH - 1)
            dve.wait_ge(rounded, 4)
            nc.vector.scalar_tensor_tensor(out=w_aug[:], in0=aug_round[:].bitcast(F32), scalar=coef[:, 1:2],
                                           in1=aug_part[:], op0=ALU.mult, op1=ALU.add).then_inc(ffn_w_ready, 1)
            nc.vector.tensor_copy(b2_aug[:, 0:E], b2_round[:, 0:E].bitcast(F32)).then_inc(ffn_w_ready, 1)
            nc.vector.tensor_tensor(b2_aug[:, E:2 * E], b2_raw[:, E:2 * E], b2_round[:, E:2 * E].bitcast(F32),
                                    ALU.subtract).then_inc(ffn_w_ready, 1)

            def bank(b):
                return ps[:, b, :].rearrange("c (r h d) -> c r h d", r=R, h=NH)

            def bias_of(n):
                return biases[:, n, :].unsqueeze(1).to_broadcast([P, R, E])

            def flat(t):
                return t.rearrange("c r h d -> c r (h d)")

            def keys_queries(s, p):
                dve.wait_ge(k_ps, s + 1)
                nc.vector.tensor_tensor(flat(kb[:, p]), rows(ps, B_K), bias_of(2), ALU.add).then_inc(kb_ready, 1)
                dve.wait_ge(kb_ready, s + 1)
                nc.vector.tensor_reduce(kmax_h[:, p].rearrange("c (r d) -> c r d", r=R),
                                        kb[:, p].rearrange("c r h d -> c r d h"), AX.X, ALU.max)\
                    .then_inc(kmaxh_ready, 1)
                dve.wait_ge(q_ps, s + 1)
                nc.vector.tensor_tensor(flat(qb[:, p]), rows(ps, B_Q), bias_of(1), ALU.add).then_inc(qb_ready, 1)
                dve.wait_ge(qb_ready, s + 1)
                nc.vector.tensor_reduce(qmax[:, p], qb[:, p].rearrange("c r h d -> c h r d"), AX.XY, ALU.max)\
                    .then_inc(qmax_ready, 1)

            def context(s, p):
                dve.wait_ge(ctx_ps, s + 1)
                chain.link(nc.vector.reciprocal(kinv[:, p:p + 1], ps[:, B_CTX, E:E + 1]))
                nc.vector.tensor_scalar(ctx_bd[0:E, p, 0:E], ps[0:E, B_CTX, 0:E], kinv[0:E, p:p + 1], float(HD),
                                        ALU.mult, ALU.mult).then_inc(ctx_ready, 1)
                nc.vector.tensor_scalar(ctx_bd[E:P, p, E:P], ps[E:P, B_CTX, 0:E], kinv[E:P, p:p + 1], float(HD),
                                        ALU.mult, ALU.mult).then_inc(ctx_ready, 1)

            def keys_values(s, p):
                dve.wait_ge(kmaxt_ps, s + 1)
                chain.link(nc.vector.tensor_reduce(kmax[:, p:p + 1], ps[0:E, B_KMAX, 0:P], AX.X, ALU.max))
                nc.vector.tensor_scalar(kdiag[:], ident[0:E, 0:E], kmax[:, p:p + 1], None, ALU.mult)\
                    .then_inc(kdiag_ready, 1)
                dve.wait_ge(v_ps, s + 1)
                nc.vector.tensor_tensor(vb[:, p, :, 0:E].rearrange("c h (r d) -> c r h d", r=R), bank(B_V),
                                        biases[:, 3, :].rearrange("c (h d) -> c h d", h=NH).unsqueeze(1)
                                        .to_broadcast([P, R, NH, HD]), ALU.add).then_inc(vb_ready, 1)
                dve.wait_ge(kbc_ps, s + 1)
                nc.vector.tensor_tensor(kb[:, p], kb[:, p],
                                        ps[:, B_KMAX, P:P + E].rearrange("c (r d) -> c r d", r=R).unsqueeze(2)
                                        .to_broadcast([P, R, NH, HD]), ALU.subtract).then_inc(ksub_done, 1)

            def attended(s, p):
                dve.wait_ge(att_ps, s + 1)
                nc.vector.reciprocal(qinv[:, p], ps[:, B_CTX, QS:QS + NH]).then_inc(qinv_ready, 1)
                dve.wait_ge(qinv_ready, s + 1)
                nc.vector.tensor_tensor(att[:, p], ps[:, B_ATT, :].rearrange("c (h f) -> c h f", h=NH),
                                        qinv[:, p].unsqueeze(2).to_broadcast([P, NH, E]), ALU.mult)\
                    .then_inc(att_ready, 1)

            def step(s, p):
                keys_queries(s, p)
                context(s - 1, 1 - p)
                keys_values(s, p)
                attended(s - 1, 1 - p)

            keys_queries(0, 0)
            keys_values(0, 0)
            base, per = chain.value, 2
            with dve.Fori(0, 3) as i:
                chain.value = base + i * (2 * per)
                step(2 * i + 1, 1)
                step(2 * i + 2, 0)
            chain.value = base + 6 * per
            step(7, 1)
            context(7, 1)
            attended(7, 1)

            def slab(u):
                return h2[:].rearrange("a j r e -> a (j r) e")[:, bass.ds(u * GT, GT), :]

            def centre(u, p):
                chain.link(nc.vector.tensor_reduce(s1b[:, p], slab(u), AX.X, ALU.add))
                nc.vector.scalar_tensor_tensor(out=xc2[:, p], in0=s1b[:, p].unsqueeze(2).to_broadcast([P, GT, E]),
                                               scalar=-1.0 / E, in1=slab(u), op0=ALU.mult, op1=ALU.add)\
                    .then_inc(xc2_ready, 1)

            def variance2(u, p):
                dve.wait_ge(sq2_ready, u + 1)
                chain.link(nc.vector.tensor_reduce(s2b[:, p], sq2[:, p], AX.X, ALU.add))
                nc.vector.tensor_scalar(var2[:, p], s2b[:, p], 1.0 / E, EPS, ALU.mult, ALU.add)\
                    .then_inc(var2_ready, 1)

            def split_tokens(u, p):
                dve.wait_ge(xt_ready, u + 1)
                chain.link(nc.vector.tensor_copy(xhl[p][0:E], xt[:, p]))
                nc.vector.tensor_tensor(xhl[p][E:P], xt[:, p], xhl[p][0:E].bitcast(F32), ALU.subtract)\
                    .then_inc(xhl_ready, 1)

            def spread(t):
                return t.unsqueeze(2).to_broadcast([P, GT, NX])

            def top_one(scores, b, n):
                chain.link(nc.vector.tensor_reduce(best[:, 2 * n], scores[:], AX.X, ALU.max))
                chain.link(nc.vector.tensor_tensor(hit[:], scores[:], spread(best[:, 2 * n]), ALU.is_equal))
                chain.link(nc.vector.tensor_tensor(hit[:], hit[:], prio[:].unsqueeze(1).to_broadcast([P, GT, NX]),
                                                   ALU.mult))
                chain.link(nc.vector.tensor_reduce(best[:, 2 * n + 1], hit[:], AX.X, ALU.max))
                chain.link(nc.vector.tensor_tensor(pick[:, n], hit[:], spread(best[:, 2 * n + 1]), ALU.is_equal))

            def route(u, p):
                dve.wait_ge(gate_ps, u + 1)
                chain.link(nc.vector.tensor_tensor(score[:], ps[:, B_GATE, 0:GT * NX].rearrange("c (t x) -> c t x", t=GT),
                                                   bg_sb[:].unsqueeze(1).to_broadcast([P, GT, NX]), ALU.add))
                top_one(score, p, 0)
                chain.link(nc.vector.scalar_tensor_tensor(out=score2[:], in0=pick[:, 0], scalar=FAR, in1=score[:],
                                                          op0=ALU.mult, op1=ALU.add))
                top_one(score2, p, 1)
                chain.link(nc.vector.tensor_tensor(mask[:, p, :, NX:2 * NX], pick[:, 0], pick[:, 1], ALU.add))
                nc.vector.tensor_scalar(mask[:, p, :, 0:NX], mask[:, p, :, NX:2 * NX], -1.0, 1.0, ALU.mult, ALU.add)\
                    .then_inc(mask_ready, 1)

            def experts_copy(u, p):
                dve.wait_ge(down_ps, 4 * u + 4)
                nc.vector.tensor_copy(ys[:, p], ps[:, B_DOWN, :]).then_inc(ys_ready, 1)

            def result(u, p):
                dve.wait_ge(yt_ps, u + 1)
                yt = ps[:, B_YT, :].rearrange("c (t y) -> c t y", t=GT)
                chain.link(nc.vector.tensor_tensor(osum[:, p], yt[:, :, 0:E], slab(u), ALU.add))
                nc.vector.tensor_tensor(o_sb[:, u, :].rearrange("a (r e) -> a r e", r=GT), yt[:, :, E:2 * E],
                                        osum[:, p], ALU.add).then_inc(out_ready, 1)

            def group(u, p, done=True, prep=True, norm=True):
                if done:
                    experts_copy(u - 1, 1 - p)
                if prep:
                    if done:
                        dve.wait_ge(up_ps, 4 * u)
                    split_tokens(u + 1, 1 - p)
                if norm:
                    centre(u + 2, p)
                if prep:
                    route(u + 1, 1 - p)
                if norm:
                    variance2(u + 2, p)
                if done:
                    result(u - 1, 1 - p)

            dve.wait_ge(h2_ready, NH)
            centre(0, 0)
            centre(1, 1)
            variance2(0, 0)
            variance2(1, 1)
            split_tokens(0, 0)
            route(0, 0)
            group(0, 0, done=False)
            base, before = chain.value, chain.links
            with dve.Fori(0, 6) as i:
                chain.value = base + i * (2 * 17)
                group(2 * i + 1, 1)
                group(2 * i + 2, 0)
                assert chain.links - before == 2 * 17
            chain.value = base + 12 * 17
            group(13, 1)
            group(14, 0, norm=False)
            group(15, 1, prep=False, norm=False)
            experts_copy(15, 1)
            result(15, 1)

        @block.tensor
        def _(pe):
            pe.wait_ge(ld_ident, 16)
            pe.wait_ge(ld_w, 16 * 8)
            for n in range(4):
                mm = nc.tensor.transpose(ps[:, 7, n * E:(n + 1) * E],
                                         w_rows[:, n].rearrange("o a e -> o (a e)"), ident[0:E, 0:E])
            mm.then_inc(wt_ps, 1)
            pe.wait_ge(x_ready, 4)
            for t in range(8):
                if t == 7:
                    pe.wait_ge(wbd_ready, 2)
                for f in range(4):
                    mm = nc.tensor.transpose(ps[:, t, f * P:(f + 1) * P], x_pt[:, 4 * t + f].rearrange("m q p w -> m (q p w)"), ident[:])
                mm.then_inc(pt_ps, 1)
            pe.wait_ge(pt_act, 4)
            pe.wait_ge(pt_dve, 4)
            for g in range(NH):
                for b in range(4):
                    mm = nc.tensor.matmul(ps[:, g, :].rearrange("c (q b e) -> c b q e", q=2, b=4)[:, b],
                                          pt[:, b, g, :], w_bd[:, 0, :],
                                          start=True, stop=True)
                mm.then_inc(emb_ps, 1)

            def transpose_tokens(g, p):
                pe.wait_ge(xn_ready, g + 1)
                for b in range(4):
                    mm = nc.tensor.transpose(ps[:, B_XNT, b * P:(b + 1) * P], xn[:, p, b * P:(b + 1) * P], ident[:])
                mm.then_inc(xnt_ps, 1)

            def project(p, bank, n, done):
                for b in range(4):
                    mm = nc.tensor.matmul(ps[:, bank, b * P:(b + 1) * P], xnt[:, p, b, :], w_bd[:, n, :],
                                          start=True, stop=True)
                mm.then_inc(done, 1)

            def keys_max(s, p):
                pe.wait_ge(kmaxh_ready, s + 1)
                pe.nop(nofuse=True)
                nc.tensor.transpose(ps[0:E, B_KMAX, 0:P], kmax_h[:, p], ident[:]).then_inc(kmaxt_ps, 1)

            def keys_max_spread(s):
                pe.wait_ge(kdiag_ready, s + 1)
                nc.tensor.matmul(ps[:, B_KMAX, P:P + E], ones_row[:], kdiag[:], start=True, stop=True)\
                    .then_inc(kbc_ps, 1)

            def transpose_queries(s, p):
                pe.wait_ge(eq_ready, s + 1)
                for n in range(4):
                    mm = nc.tensor.transpose(ps[:, B_EQT, n * P:(n + 1) * P],
                                             eq[:, p, 2 * n:2 * n + 2, :].rearrange("c h f -> c (h f)"), ident[:])
                mm.then_inc(eqt_ps, 1)

            def context(s, p):
                pe.wait_ge(ek_ready, s + 1)
                pe.wait_ge(vb_ready, s + 1)
                for h in range(NH):
                    for half in range(2):
                        mm = nc.tensor.matmul(ps[half * E:(half + 1) * E, B_CTX, 0:E + 1], ek[:, p, h, :],
                                              vb[:, p, h, :], start=(h == 0), stop=(h == NH - 1))
                mm.then_inc(ctx_ps, 1)

            def attend(s, p):
                pe.wait_ge(eqt_ready, s + 1)
                pe.wait_ge(ctx_ready, 2 * (s + 1))
                for n in range(4):
                    nc.tensor.matmul(ps[:, B_ATT, n * P:(n + 1) * P], eqt[:, p, n, :], ctx_bd[:, p, :],
                                     start=True, stop=True)
                    mm = nc.tensor.matmul(ps[:, B_CTX, QS + 2 * n:QS + 2 * n + 2], eqt[:, p, n, :], ones_bd[:],
                                          start=True, stop=True)
                mm.then_inc(att_ps, 1)

            def step(s, p, first=False, last=False):
                pe.wait_ge(xnt_ready, s + 1)
                if not first:
                    pe.wait_ge(kb_ready, s)
                project(p, B_K, 2, k_ps)
                if not first:
                    pe.wait_ge(qb_ready, s)
                project(p, B_Q, 1, q_ps)
                if not first:
                    pe.wait_ge(vb_ready, s)
                project(p, B_V, 3, v_ps)
                if not first:
                    pe.wait_ge(kb_ready, s + 1)
                    context(s - 1, 1 - p)
                if not first:
                    pe.wait_ge(ksub_done, s)
                keys_max(s, p)
                if not last:
                    transpose_tokens(s + 1, 1 - p)
                keys_max_spread(s)
                if not first:
                    pe.wait_ge(eqt_ready, s)
                transpose_queries(s, p)
                if not first:
                    attend(s - 1, 1 - p)

            pe.wait_ge(h_ready, NH)
            transpose_tokens(0, 0)
            step(0, 0, first=True)
            with pe.Fori(0, 3) as i:
                step(2 * i + 1, 1)
                step(2 * i + 2, 0)
            step(7, 1, last=True)
            pe.wait_ge(qinv_ready, 7)
            context(7, 1)
            attend(7, 1)

            def transpose2(u, p):
                pe.wait_ge(xn2_ready, u + 1)
                pe.nop(nofuse=True)
                for t in range(GT):
                    mm = nc.tensor.transpose(ps[0:E, B_T, t * P:(t + 1) * P], xn2[:, p, t, :], ident[:])
                mm.then_inc(xt_ps, 1)

            def gate(u, p):
                pe.wait_ge(xt_ready, u + 1)
                for t in range(GT):
                    mm = nc.tensor.matmul(ps[:, B_GATE, t * NX:(t + 1) * NX], xt[:, p, t * P:(t + 1) * P], wg_sb[:],
                                          start=True, stop=True)
                mm.then_inc(gate_ps, 1)

            def transpose_mask(u, p):
                pe.wait_ge(mask_ready, u + 1)
                for t in range(GT):
                    mm = nc.tensor.transpose(ps[0:NM, B_GATE, t * P:(t + 1) * P], mask[:, p, t, :], ident[:])
                mm.then_inc(mask_ps, 1)

            def up(u, p, pair, wait_bank=True):
                if wait_bank:
                    pe.wait_ge(hid_ready, 4 * u + pair - 1)
                for k in range(2):
                    e = 2 * pair + k
                    bank = 2 * (pair % 2) + k
                    nc.tensor.matmul(ps[:, bank, :], w1_hh[:, e, :], xhl[p][:], start=True, stop=False)
                    mm = nc.tensor.matmul(ps[:, bank, :], w_aug[:, e * HID:(e + 1) * HID], xm[p][:],
                                          start=False, stop=True)
                mm.then_inc(up_ps, 1)

            def down(u, pair):
                pe.wait_ge(hid_ready, 4 * u + pair + 1)
                for k in range(2):
                    mm = nc.tensor.matmul(ps[k * E:(k + 1) * E, B_DOWN, :], w2_sb[:, 2 * pair + k, :],
                                          hid[:, pair % 2, k, :], start=False, stop=(pair == 3),
                                          skip_group_check=True)
                mm.then_inc(down_ps, 1)

            def down_bias(u, p):
                nc.tensor.matmul(ps[:, B_DOWN, :], b2_aug[:], xm[p][:], start=True, stop=False,
                                 skip_group_check=True)

            def transpose_result(u, p):
                pe.wait_ge(ys_ready, u + 1)
                for t in range(GT):
                    mm = nc.tensor.transpose(ps[:, B_YT, t * P:(t + 1) * P], ys[:, p, t * P:(t + 1) * P], ident[:])
                mm.then_inc(yt_ps, 1)

            def group(u, p, first=False, prep=True):
                if prep:
                    pe.wait_ge(xmx_ready, u + 1)
                    transpose2(u + 1, 1 - p)
                pe.wait_ge(xhl_ready, u + 1)
                pe.wait_ge(xmm_ready, u + 1)
                up(u, p, 0, not first)
                if not first:
                    down(u - 1, 3)
                if prep:
                    gate(u + 1, 1 - p)
                up(u, p, 1, not first)
                if not first:
                    pe.wait_ge(ys_ready, u)
                down_bias(u, p)
                down(u, 0)
                up(u, p, 2)
                down(u, 1)
                if not first:
                    transpose_result(u - 1, 1 - p)
                if prep:
                    transpose_mask(u + 1, 1 - p)
                up(u, p, 3)
                down(u, 2)

            pe.wait_ge(att_ready, NH)
            pe.wait_ge(ld_ffn, 16 * 13)
            transpose2(0, 0)
            gate(0, 0)
            transpose_mask(0, 0)
            pe.wait_ge(ffn_w_ready, 3)
            group(0, 0, first=True)
            with pe.Fori(0, 6) as i:
                group(2 * i + 1, 1)
                group(2 * i + 2, 0)
            group(13, 1)
            group(14, 0)
            group(15, 1, prep=False)
            down(15, 3)
            transpose_result(15, 1)


_INS = ['x', 'L0_tok_W', 'L0_tok_b', 'L0_tok_pos_embed', 'L0_attn_Wq', 'L0_attn_bq', 'L0_attn_Wk', 'L0_attn_bk',
        'L0_attn_Wv', 'L0_attn_bv', 'L0_ffn_Wg', 'L0_ffn_bg', 'L0_ffn_W1', 'L0_ffn_b1', 'L0_ffn_W2', 'L0_ffn_b2']


def _constants(np):
    rows = np.zeros((16, NX, HID), np.float32)
    for e in range(NX):
        rows[e, e, :] = -BIG
    coef = np.zeros((KM, 2), np.float32)
    coef[0:E] = (1.0, -1.0)
    coef[E:E + 16] = (1.0, 0.0)
    coef[E + 16] = (0.0, 1.0)
    coef[E + 17] = (1.0, -1.0)
    prio = np.tile(np.arange(NX, 0, -1, dtype=np.float32), (P, 1))
    return {"ident": np.eye(P, dtype=np.float32), "rows": rows.reshape(16, NX * HID), "coef": coef, "prio": prio}


def kernel(**inputs):
    import numpy as _np
    import concourse.bacc as _bacc
    from concourse import mybir as _mybir
    from concourse.bass_utils import run_bass_kernel_spmd as _run

    nc = _bacc.Bacc("TRN2", target_bir_lowering=False, num_devices=1)
    arrays, args = {}, []
    for name in _INS:
        a = _np.ascontiguousarray(inputs[name])
        arrays[f"in_{name}_dram"] = a
        args.append(nc.dram_tensor(f"in_{name}_dram", a.shape, _mybir.dt.from_np(a.dtype), kind="ExternalInput").ap())
    for name, a in _constants(_np).items():
        arrays[f"const_{name}_dram"] = a
        args.append(nc.dram_tensor(f"const_{name}_dram", a.shape, _mybir.dt.from_np(a.dtype), kind="ExternalInput").ap())
    args.append(nc.dram_tensor("out_0_dram", (R, C, E), _mybir.dt.float32, kind="ExternalOutput").ap())
    bass_vit_layer_kernel(nc, *args)
    r = _run(nc, [arrays], core_ids=[0])
    return r.results[0]["out_0_dram"]
```

```python
from contextlib import ExitStack

import concourse.bass as bass
from concourse import mybir

F32 = mybir.dt.float32
F32R = mybir.dt.float32r
ALU = mybir.AluOpType
ACT = mybir.ActivationFunctionType
AX = mybir.AxisListType

P = 128
R = 8
C = 1024
E = 64
NH = 8
HD = E // NH
PATCH = 8
ROW = R * E
NX = 8
HID = 128
NG = 16
GT = 4
GW = GT * E
NM = 18
KM = E + NM
EPS = 1e-5
BIG = float(2 ** 100)
FAR = -3.0e38


class Chain:

    def __init__(self, eng, sem):
        self.eng, self.sem, self.value, self.links = eng, sem, 0, 0

    def link(self, ins):
        self.value = self.value + 1
        self.links += 1
        ins.then_inc(self.sem, 1)
        self.eng.wait_ge(self.sem, self.value)


def bass_vit_layer_kernel(nc, x, tok_w, tok_b, pos, wq, bq, wk, bk, wv, bv, wg, bg, w1, b1, w2, b2,
                          c_ident, c_rows, c_coef, c_prio, c_bias, out):
    h_dram = nc.dram_tensor("residual_by_patch", (C, ROW), F32, kind="Internal").ap()

    with ExitStack() as ctx:
        def sb(name, shape, dt=F32):
            return ctx.enter_context(nc.sbuf_tensor(name, shape, dt))

        def sem(name):
            return ctx.enter_context(nc.semaphore(name))

        ident = sb("ident", [P, P])
        w_rows = sb("w_rows", [E, 4, 2, E])
        w_bd = sb("w_bd", [P, 4, P])
        tokb_sb = sb("tokb_sb", [P, E])
        ones_row = sb("ones_row", [E, P])
        bias_raw = sb("bias_raw", [P, 3, E])
        bias_round = sb("bias_round", [P, 3, E], F32R)
        bias_part = sb("bias_part", [P, 3, E])
        bias_rows = sb("bias_rows", [P, 3, E], F32R)
        bias_coef = sb("bias_coef", [P, 2])
        bias_sel = sb("bias_sel", [P, P], F32R)
        minus_half = sb("minus_half", [P, 8])
        gelu_first = sb("gelu_first", [P, 8])
        w1_raw = sb("w1_raw", [P, NX, HID])
        w1_hh = sb("w1_hh", [P, NX, HID], F32R)
        aug_raw = sb("aug_raw", [KM, NX * HID])
        aug_round = sb("aug_round", [KM, NX * HID], F32R)
        aug_part = sb("aug_part", [KM, NX * HID])
        w_aug = sb("w_aug", [KM, NX * HID], F32R)
        coef = sb("coef", [KM, 2])
        b2_raw = sb("b2_raw", [KM, 2 * E])
        b2_round = sb("b2_round", [KM, 2 * E], F32R)
        b2_aug = sb("b2_aug", [KM, 2 * E], F32R)
        w2_sb = sb("w2_sb", [HID, NX, E])
        wg_raw = sb("wg_raw", [P, NX])
        wg_hl = sb("wg_hl", [P, 2 * NX], F32R)
        bg_sb = sb("bg_sb", [P, NX])
        prio = sb("prio", [P, NX])

        x_sb = sb("x_sb", [P, 2, PATCH, 32, PATCH])
        x_pt = sb("x_pt", [P, 32, 2, PATCH, PATCH])
        pt = sb("pt", [P, 4, NH, P])
        posb = sb("posb", [P, NH, E])
        h_sb = sb("h_sb", [P, NH, ROW])
        xc = sb("xc", [P, NH, ROW])
        sq = x_sb[:].rearrange("p q k f w -> p (q k f w)").rearrange("p (g f) -> p g f", g=NH)
        s1 = sb("s1", [P, NH, R])
        mean = sb("mean", [P, NH, R])
        s2 = sb("s2", [P, NH, R])
        var = sb("var", [P, NH, R])
        rstd = sb("rstd", [P, NH, R])

        xn = xc
        xnt = x_pt[:].rearrange("p f q k w -> p (f q k w)").rearrange("p (g b c) -> p g b c", g=NH, b=4)
        kmax_h = sb("kmax_h", [P, 2, E])
        kmax = sb("kmax", [E, 2])
        kdiag = sb("kdiag", [E, E])
        kmax_all = sb("kmax_all", [P, E])
        kb = sb("kb", [P, 2, R, NH, HD])
        qb = sb("qb", [P, 2, R, NH, HD])
        eq = sb("eq", [P, 2, NH, E])
        ek = sb("ek", [P, 2, NH, E])
        vb = sb("vb", [P, 2, NH, E + 1])
        qmax = sb("qmax", [P, 2, NH])
        qsum = sb("qsum", [P, 2, NH])
        qinv = sb("qinv", [P, 2, NH])
        kinv = sb("kinv", [P, 2])
        ctx_bd = sb("ctx_bd", [P, 2, P])
        eqt = sb("eqt", [P, 2, 4, P])
        att = sb("att", [P, NH * R, E])
        h2 = sb("h2", [P, NH, R, E])

        xc2 = sb("xc2", [P, 2, GT, E])
        sq2 = sb("sq2", [P, 2, GT, E])
        s1b = sb("s1b", [P, 2, GT])
        s2b = sb("s2b", [P, 2, GT])
        var2 = sb("var2", [P, 2, GT])
        rstd2 = sb("rstd2", [P, 2, GT])
        xn2 = sb("xn2", [P, 2, GT, E])
        xhl = [sb(f"xhl{n}", [P, 512], F32R) for n in range(2)]
        xm = [sb(f"xm{n}", [KM, 512], F32R) for n in range(2)]
        score = sb("score", [P, GT, NX])
        score2 = sb("score2", [P, GT, NX])
        hit = sb("hit", [P, GT, NX])
        pick = sb("pick", [P, 2, GT, NX])
        best = sb("best", [P, 4, GT])
        mask = sb("mask", [P, 2, GT, 32])
        hid = sb("hid", [HID, 2, 2, 512])
        aug_minus = hid[0:KM].rearrange("k a b c -> k (a b c)")[:, 0:NX * HID]
        ys = sb("ys", [P, 2, 512])
        osum = sb("osum", [P, GT, E])
        o_sb = xc[:].rearrange("p g (t f) -> p (g t) f", t=2)

        ps = ctx.enter_context(nc.psum_tensor("ps", [P, 8, 512], F32))

        ld_ident, ld_w, ld_bias = sem("ld_ident"), sem("ld_w"), sem("ld_bias")
        ld_x = [[sem(f"ld_x{part}_{n}") for n in range(4)] for part in range(2)]
        x_ready = [sem("x_ready_left"), sem("x_ready_right")]
        ld_ffn, ld_qkvb = sem("ld_ffn"), sem("ld_qkvb")
        res_out, res_in = sem("res_out"), sem("res_in")
        stored = [sem("stored_even"), sem("stored_odd")]
        zeroed, wt_ps, wbd_ready, posb_ready = sem("zeroed"), sem("wt_ps"), sem("wbd_ready"), sem("posb_ready")
        pt_ps, pt_act, pt_dve = sem("pt_ps"), sem("pt_act"), sem("pt_dve")
        rounded, ffn_w_ready, biasr_ready = sem("rounded"), sem("ffn_w_ready"), sem("biasr_ready")
        bias_rounded = sem("bias_rounded")
        emb_ps, h_ready, xc_ready, sq_ready = sem("emb_ps"), sem("h_ready"), sem("xc_ready"), sem("sq_ready")
        mean_ready, var_ready, rstd_ready = sem("mean_ready"), sem("var_ready"), sem("rstd_ready")
        xn_ready, xnt_ps, xnt_ready = sem("xn_ready"), sem("xnt_ps"), sem("xnt_ready")
        q_ps, qmax_ready, qsub_done, eq_ready = sem("q_ps"), sem("qmax_ready"), sem("qsub_done"), sem("eq_ready")
        eqt_ps, eqt_ready, qinv_ready = sem("eqt_ps"), sem("eqt_ready"), sem("qinv_ready")
        k_ps, kmaxh_ready, kmaxt_ps, kdiag_ready = sem("k_ps"), sem("kmaxh_ready"), sem("kmaxt_ps"), sem("kdiag_ready")
        kmaxb_ps, kmaxb_ready, ksub_done, ek_ready = sem("kmaxb_ps"), sem("kmaxb_ready"), sem("ksub_done"), sem("ek_ready")
        v_ps, vb_ready, ctx_ps, kinv_ready, ctx_ready = sem("v_ps"), sem("vb_ready"), sem("ctx_ps"), sem("kinv_ready"), sem("ctx_ready")
        att_ps, att_ready = sem("att_ps"), sem("att_ready")
        xc2_ready, sq2_ready, var2_ready, rstd2_ready = sem("xc2_ready"), sem("sq2_ready"), sem("var2_ready"), sem("rstd2_ready")
        xn2_ready, xt_ps, xh_ready, xmx_ready = sem("xn2_ready"), sem("xt_ps"), sem("xh_ready"), sem("xmx_ready")
        xhl_ready, gate_ps, score_read, mask_ready = sem("xhl_ready"), sem("gate_ps"), sem("score_read"), sem("mask_ready")
        mask_ps, xmm_ready = sem("mask_ps"), sem("xmm_ready")
        up_ps, hid_ready, down_ps = sem("up_ps"), sem("hid_ready"), sem("down_ps")
        ys_ready, yt_ps, out_ready = sem("ys_ready"), sem("yt_ps"), sem("out_ready")
        dve_chain = sem("dve_chain")

        block = ctx.enter_context(nc.Block())

        STEPS = range(-2, NH + 1)

        def at_block(stage, g):
            if 0 <= g < NH:
                stage(g)

        B_EMB, B_K, B_Q, B_V, B_KMAX, B_CTX, B_EQT, B_ATT = range(8)
        B_DOWN, B_T, B_GATE, B_YT = 4, 5, 6, 7

        def tiles(t, odd):
            return t.rearrange("k (t o c) -> k o t c", o=2, c=P)[:, odd]

        def tiles_ps(odd):
            return ps[odd * E:(odd + 1) * E, B_T, 0:2 * P].rearrange("k (t c) -> k t c", t=2)

        def load_x(eng, fh):
            images = x.rearrange("(q b) o (m p) c -> q (b o m) p c", q=2, p=PATCH)
            for part in range(2):
                for q in range(2):
                    at = fh * 256 + part * 128
                    eng.dma_start(x_sb[fh * 64:(fh + 1) * 64, q, :, part * 16:(part + 1) * 16, :]
                                  .rearrange("m p f w -> m p (f w)"),
                                  images[q, :, :, at:at + 128]).then_inc(ld_x[part][2 * fh + q], 16)

        def regroup_x(eng, copy, part, fh, q):
            at, f = slice(fh * 64, (fh + 1) * 64), slice(part * 16, (part + 1) * 16)
            eng.wait_ge(ld_x[part][2 * fh + q], 16)
            copy(x_pt[at, f, q].rearrange("m f p w -> m p f w"), x_sb[at, q, :, f]).then_inc(x_ready[part], 1)

        def patches_out(t):
            return (pt[:].rearrange("k b g (m a f) -> k f a (b g m)", m=2, a=2)[:, 4 * t:4 * t + 4],
                    ps[:, t, :].rearrange("k (f a c) -> k f a c", f=4, a=2))

        @block.sync
        def _(sp):
            sp.dma_start(ident[:], c_ident).then_inc(ld_ident, 16)
            load_x(sp, 0)
            sp.dma_start(tokb_sb[:], tok_b.partition_broadcast(P)).then_inc(ld_bias, 16)
            sp.dma_start(posb[:], pos[0].rearrange("(g c) e -> c g e", g=NH)).then_inc(ld_bias, 16)
            sp.wait_ge(zeroed, 2)
            for n, b in enumerate((bq, bk, bv)):
                for row in range(2):
                    sp.dma_start(bias_raw[row:row + 1, n, :], b.rearrange("(a e) -> a e", a=1)).then_inc(ld_qkvb, 16)
            sp.dma_start(bias_coef[:], c_bias).then_inc(ld_qkvb, 16)
            w1_in = w1.rearrange("x d h -> d x h")
            for half in range(2):
                sp.dma_start(w1_raw[half * E:(half + 1) * E], w1_in).then_inc(ld_ffn, 16)
            sp.dma_start(aug_raw[0:E].rearrange("d (x h) -> d x h", x=NX), w1_in).then_inc(ld_ffn, 16)
            sp.dma_start(aug_raw[E:E + 16], c_rows).then_inc(ld_ffn, 16)
            for n in range(2):
                sp.dma_start(aug_raw[E + 16 + n:E + 17 + n],
                             b1.rearrange("(a x) h -> a (x h)", a=1)).then_inc(ld_ffn, 16)
            for n in range(2):
                sp.dma_start(b2_raw[E + 8:E + 16, n * E:(n + 1) * E], b2).then_inc(ld_ffn, 16)
            sp.dma_start(coef[:], c_coef).then_inc(ld_ffn, 16)
            sp.dma_start(w2_sb[:], w2.rearrange("x h d -> h x d")).then_inc(ld_ffn, 16)
            for half in range(2):
                sp.dma_start(wg_raw[half * E:(half + 1) * E], wg).then_inc(ld_ffn, 16)
            sp.dma_start(bg_sb[:], bg.partition_broadcast(P)).then_inc(ld_ffn, 16)
            sp.dma_start(prio[:], c_prio).then_inc(ld_ffn, 16)
            res_rows = h_dram.rearrange("(g c) f -> g c f", g=NH)
            with sp.Fori(0, NH) as g:
                sp.wait_ge(h_ready, g + 1)
                sp.dma_start(res_rows[g], h_sb[:, g, :]).then_inc(res_out, 16)
            sp.wait_ge(res_out, 16 * NH)
            sp.dma_start(h2[:].rearrange("a j r e -> a (j r e)"),
                         h_dram.rearrange("(a j) f -> a (j f)", j=8)).then_inc(res_in, 16)
            out_v = out.rearrange("r (a j) e -> j a r e", j=8)
            with sp.Fori(0, NG // 2) as j:
                for half in range(2):
                    sp.wait_ge(out_ready, 2 * j + half + 1)
                    sp.dma_start(out_v[j, :, GT * half:GT * (half + 1), :],
                                 o_sb[:, 2 * j + half, :].rearrange("a (r e) -> a r e", r=GT)).then_inc(stored[half], 16)
            for half in range(2):
                sp.wait_ge(stored[half], 16 * (NG // 2))

        @block.gpsimd
        def _(pool):
            for n, w in enumerate((tok_w, wq, wk, wv)):
                pool.dma_start(w_rows[:, n], w.unsqueeze(1).to_broadcast([E, 2, E])).then_inc(ld_w, 16)
            nc.gpsimd.memset(bias_raw[:], 0.0).then_inc(zeroed, 1)
            nc.gpsimd.memset(b2_raw[:], 0.0).then_inc(zeroed, 1)
            nc.gpsimd.memset(w_bd[:], 0.0).then_inc(zeroed, 1)
            nc.gpsimd.memset(minus_half[:], -0.5).then_inc(zeroed, 1)
            pool.wait_ge(zeroed, 4)
            nc.gpsimd.memset(ctx_bd[:], 0.0).then_inc(zeroed, 1)
            nc.gpsimd.memset(ones_row[:], 1.0).then_inc(zeroed, 1)
            nc.gpsimd.memset(vb[:], float(HD) ** -1.0).then_inc(zeroed, 1)
            nc.gpsimd.memset(mask[:], 1.0).then_inc(zeroed, 1)
            nc.gpsimd.memset(bias_sel[:].bitcast(F32), 0.0).then_inc(zeroed, 1)
            pool.wait_ge(zeroed, 9)
            nc.gpsimd.memset(bias_sel[0:2, :].bitcast(F32), 1.0).then_inc(zeroed, 1)
            pool.wait_ge(zeroed, 10)
            pool.wait_ge(ld_bias, 16 * 2)
            nc.gpsimd.tensor_tensor(posb[:], posb[:], tokb_sb[:].unsqueeze(1).to_broadcast([P, NH, E]),
                                    ALU.add).then_inc(posb_ready, 1)
            for g in range(NH):
                if g >= 2:
                    pool.wait_ge(mean_ready, g - 1)
                    nc.gpsimd.tensor_tensor(xc[:, g, :].rearrange("c (r e) -> c r e", r=R),
                                            h_sb[:, g, :].rearrange("c (r e) -> c r e", r=R),
                                            mean[:, g, :].unsqueeze(2).to_broadcast([P, R, E]), ALU.subtract)\
                        .then_inc(xc_ready, 1)
                pool.wait_ge(var_ready, g + 1)
                nc.gpsimd.tensor_tensor(rstd[:, g, :], var[:, g, :], minus_half[:], ALU.pow).then_inc(rstd_ready, 1)
                pool.wait_ge(rstd_ready, g + 1)
                nc.gpsimd.tensor_tensor(xn[:, g, :].rearrange("c (r e) -> c r e", r=R),
                                        xc[:, g, :].rearrange("c (r e) -> c r e", r=R),
                                        rstd[:, g, :].unsqueeze(2).to_broadcast([P, R, E]), ALU.mult)\
                    .then_inc(xn_ready, 1)

            pool.wait_ge(rounded, 6)
            nc.gpsimd.tensor_tensor(w_aug[:], aug_part[:], aug_minus, ALU.add).then_inc(ffn_w_ready, 1)

            def norm2(u, p, first=False):
                pool.wait_ge(var2_ready, u + 1)
                nc.gpsimd.tensor_tensor(rstd2[:, p], var2[:, p], minus_half[:, 0:GT], ALU.pow)\
                    .then_inc(rstd2_ready, 1)
                pool.wait_ge(rstd2_ready, u + 1)
                if not first:
                    pool.wait_ge(xt_ps, u - 1)
                nc.gpsimd.tensor_tensor(xn2[:, p], xc2[:, p],
                                        rstd2[:, p].unsqueeze(2).to_broadcast([P, GT, E]), ALU.mult)\
                    .then_inc(xn2_ready, 1)

            def tokens_again(u, p):
                pool.wait_ge(xh_ready, 2 * u + 2)
                pool.nop(nofuse=True)
                nc.gpsimd.tensor_copy(xm[p][0:E], xhl[p][0:E].bitcast(F32)).then_inc(xmx_ready, 1)

            def group(u, p):
                pool.wait_ge(up_ps, 4 * u)
                tokens_again(u + 1, 1 - p)
                norm2(u + 3, 1 - p)

            norm2(0, 0, first=True)
            norm2(1, 1, first=True)
            tokens_again(0, 0)
            norm2(2, 0)
            tokens_again(1, 1)
            norm2(3, 1)
            with pool.Fori(0, 6) as i:
                group(2 * i + 1, 1)
                group(2 * i + 2, 0)
            for u in (13, 14):
                pool.wait_ge(up_ps, 4 * u)
                tokens_again(u + 1, (u + 1) % 2)

        @block.scalar
        def _(act):
            load_x(act, 1)
            for t in range(1, 8, 2):
                act.wait_ge(pt_ps, t + 1)
                dst, src = patches_out(t)
                nc.scalar.activation(dst, src, ACT.Copy).then_inc(pt_act, 1)
            act.wait_ge(ld_qkvb, 16 * 7)
            nc.scalar.activation(bias_round[:], bias_raw[:], ACT.Copy).then_inc(bias_rounded, 1)
            nc.scalar.activation(bias_part[:], bias_raw[:], ACT.Copy, scale=bias_coef[:, 0:1]).then_inc(bias_rounded, 1)

            def squares1(g):
                act.wait_ge(xc_ready, g + 1)
                nc.scalar.activation(sq[:, g, :], xc[:, g, :], ACT.Square).then_inc(sq_ready, 1)

            def tokens1(g):
                act.wait_ge(xnt_ps, g + 1)
                nc.scalar.activation(xnt[:, g].rearrange("k b c -> k (b c)"), ps[:, B_EMB, :], ACT.Copy)\
                    .then_inc(xnt_ready, 1)

            def exp_queries(g):
                act.wait_ge(qsub_done, g + 1)
                nc.scalar.activation(eq[:, g % 2].rearrange("c h (r d) -> c r h d", r=R), qb[:, g % 2], ACT.Exp)\
                    .then_inc(eq_ready, 1)

            def keys_max_copy(g):
                act.wait_ge(kmaxb_ps, g + 1)
                nc.scalar.activation(kmax_all[:], ps[:, B_KMAX, P:P + E], ACT.Copy).then_inc(kmaxb_ready, 1)

            def values(g):
                act.wait_ge(v_ps, g + 1)
                nc.scalar.activation(vb[:, g % 2, :, 0:E].rearrange("c h (r d) -> c r h d", r=R),
                                     ps[:, B_V, :].rearrange("c (r h d) -> c r h d", r=R, h=NH), ACT.Copy)\
                    .then_inc(vb_ready, 1)

            def exp_keys(g):
                act.wait_ge(ksub_done, g + 1)
                nc.scalar.activation(ek[:, g % 2].rearrange("c h (r d) -> c r h d", r=R), kb[:, g % 2], ACT.Exp)\
                    .then_inc(ek_ready, 1)

            def context_scaled(g):
                act.wait_ge(kinv_ready, g + 1)
                for half in (slice(0, E), slice(E, P)):
                    nc.scalar.activation(ctx_bd[half, g % 2, half], ps[half, B_CTX, 0:E], ACT.Copy,
                                         scale=kinv[half, g % 2:g % 2 + 1]).then_inc(ctx_ready, 1)

            def queries_copy(g):
                act.wait_ge(eqt_ps, g + 1)
                nc.scalar.activation(eqt[:, g % 2].rearrange("k b c -> k (b c)"), ps[:, B_EQT, :], ACT.Copy)\
                    .then_inc(eqt_ready, 1)

            for s in STEPS:
                at_block(context_scaled, s - 1)
                at_block(exp_queries, s)
                at_block(keys_max_copy, s)
                at_block(values, s)
                at_block(tokens1, s + 1)
                at_block(squares1, s + 2)
                at_block(exp_keys, s)
                at_block(queries_copy, s)
                if s == 3:
                    act.wait_ge(ld_ffn, 16 * 14)
                    nc.scalar.activation(w1_hh[:], w1_raw[:], ACT.Copy).then_inc(rounded, 1)
                    nc.scalar.activation(aug_round[:], aug_raw[:], ACT.Copy).then_inc(rounded, 1)
                if s == 4:
                    nc.scalar.activation(aug_part[:], aug_raw[:], ACT.Copy, scale=coef[:, 0:1]).then_inc(rounded, 1)
                    nc.scalar.activation(b2_round[:], b2_raw[:], ACT.Copy).then_inc(rounded, 1)
                    nc.scalar.activation(wg_hl[:, 0:NX], wg_raw[:], ACT.Copy).then_inc(rounded, 1)
                    act.wait_ge(rounded, 2)
                    nc.scalar.activation(aug_minus, aug_round[:].bitcast(F32), ACT.Copy, scale=coef[:, 1:2])\
                        .then_inc(rounded, 1)

            def squares(u, p):
                act.wait_ge(xc2_ready, u + 1)
                nc.scalar.activation(sq2[:, p], xc2[:, p], ACT.Square).then_inc(sq2_ready, 1)

            def tokens_high(u, p):
                act.wait_ge(xt_ps, u + 1)
                for odd in range(2):
                    nc.scalar.activation(tiles(xhl[p][0:E], odd), tiles_ps(odd), ACT.Copy).then_inc(xh_ready, 1)

            def mask_copy(u, p):
                act.wait_ge(mask_ps, u + 1)
                for t in range(GT):
                    ins = nc.scalar.activation(xm[p][E:KM, t * P:(t + 1) * P], ps[32 * t:32 * t + NM, B_GATE, 0:P],
                                               ACT.Copy)
                ins.then_inc(xmm_ready, 1)

            def gelu(u, pair, wait_hid=True):
                act.wait_ge(up_ps, 4 * u + pair + 1)
                if wait_hid:
                    act.wait_ge(down_ps, 4 * u + pair - 1)
                at = 2 * (pair % 2)
                nc.scalar.activation(hid[:, pair % 2], ps[:, at:at + 2, :], ACT.Gelu).then_inc(hid_ready, 1)

            def group(u, p, first=False, prep=True, norm=True):
                if prep:
                    if not first:
                        act.wait_ge(up_ps, 4 * u)
                    tokens_high(u + 1, 1 - p)
                gelu(u, 0, not first)
                gelu(u, 1, not first)
                gelu(u, 2)
                if prep:
                    mask_copy(u + 1, 1 - p)
                if norm:
                    squares(u + 3, 1 - p)
                gelu(u, 3)

            nc.scalar.activation(gelu_first[:], minus_half[:], ACT.Gelu)
            squares(0, 0)
            squares(1, 1)
            tokens_high(0, 0)
            mask_copy(0, 0)
            squares(2, 0)
            group(0, 0, first=True)
            with act.Fori(0, 6) as i:
                group(2 * i + 1, 1)
                group(2 * i + 2, 0)
            group(13, 1, norm=False)
            group(14, 0, norm=False)
            group(15, 1, prep=False, norm=False)

        @block.vector
        def _(dve):
            chain = Chain(dve, dve_chain)
            for part in range(2):
                for q in range(2):
                    for fh in (1, 0):
                        regroup_x(dve, nc.vector.tensor_copy, part, fh, q)
            dve.wait_ge(zeroed, 4)
            dve.wait_ge(wt_ps, 1)
            wt = ps[:, 7, 0:4 * E].rearrange("k (w e) -> k w e", w=4)
            nc.vector.tensor_copy(w_bd[0:E, :, 0:E], wt[0:E]).then_inc(wbd_ready, 1)
            nc.vector.tensor_copy(w_bd[E:P, :, E:P], wt[E:P]).then_inc(wbd_ready, 1)
            for t in range(0, 8, 2):
                dve.wait_ge(pt_ps, t + 1)
                dst, src = patches_out(t)
                nc.vector.tensor_copy(dst, src).then_inc(pt_dve, 1)

            def rows(t, g):
                return t[:, g, :].rearrange("c (r e) -> c r e", r=R)

            def embed(g):
                dve.wait_ge(emb_ps, g + 1)
                nc.vector.tensor_tensor(rows(h_sb, g), rows(ps, B_EMB),
                                        posb[:, g, :].unsqueeze(1).to_broadcast([P, R, E]), ALU.add)\
                    .then_inc(h_ready, 1)
                dve.wait_ge(h_ready, g + 1)
                chain.link(nc.vector.tensor_reduce(s1[:, g, :], rows(h_sb, g), AX.X, ALU.add))
                if g < 2:
                    nc.vector.scalar_tensor_tensor(out=rows(xc, g), in0=s1[:, g, :].unsqueeze(2).to_broadcast([P, R, E]),
                                                   scalar=-1.0 / E, in1=rows(h_sb, g), op0=ALU.mult, op1=ALU.add)\
                        .then_inc(xc_ready, 1)
                else:
                    nc.vector.tensor_scalar(mean[:, g, :], s1[:, g, :], 1.0 / E, None, ALU.mult)\
                        .then_inc(mean_ready, 1)

            def variance(g):
                dve.wait_ge(sq_ready, g + 1)
                chain.link(nc.vector.tensor_reduce(s2[:, g, :], rows(sq, g), AX.X, ALU.add))
                nc.vector.tensor_scalar(var[:, g, :], s2[:, g, :], 1.0 / E, EPS, ALU.mult, ALU.add)\
                    .then_inc(var_ready, 1)

            def bank(b):
                return ps[:, b, :].rearrange("c (r h d) -> c r h d", r=R, h=NH)

            def queries_max(g):
                dve.wait_ge(q_ps, g + 1)
                nc.vector.tensor_reduce(qmax[:, g % 2], bank(B_Q).rearrange("c r h d -> c h r d"), AX.XY, ALU.max)\
                    .then_inc(qmax_ready, 1)

            def queries_minus_max(g):
                dve.wait_ge(qmax_ready, g + 1)
                nc.vector.tensor_tensor(qb[:, g % 2], bank(B_Q),
                                        qmax[:, g % 2].unsqueeze(1).unsqueeze(3).to_broadcast([P, R, NH, HD]),
                                        ALU.subtract).then_inc(qsub_done, 1)

            def keys_max_of_h(g):
                dve.wait_ge(k_ps, g + 1)
                nc.vector.tensor_reduce(kmax_h[:, g % 2].rearrange("c (r d) -> c r d", r=R),
                                        bank(B_K).rearrange("c r h d -> c r d h"), AX.X, ALU.max)\
                    .then_inc(kmaxh_ready, 1)

            def keys_max(g):
                dve.wait_ge(kmaxt_ps, g + 1)
                chain.link(nc.vector.tensor_reduce(kmax[:, g % 2:g % 2 + 1], ps[0:E, B_KMAX, 0:P], AX.X, ALU.max))
                nc.vector.tensor_scalar(kdiag[:], ident[0:E, 0:E], kmax[:, g % 2:g % 2 + 1], None, ALU.mult)\
                    .then_inc(kdiag_ready, 1)

            def keys_minus_max(g):
                dve.wait_ge(kmaxb_ready, g + 1)
                nc.vector.tensor_tensor(kb[:, g % 2], bank(B_K),
                                        kmax_all[:].rearrange("c (r d) -> c r d", r=R).unsqueeze(2)
                                        .to_broadcast([P, R, NH, HD]), ALU.subtract).then_inc(ksub_done, 1)

            def keys_inverse(g):
                dve.wait_ge(ctx_ps, g + 1)
                nc.vector.reciprocal(kinv[:, g % 2:g % 2 + 1], ps[:, B_CTX, E:E + 1]).then_inc(kinv_ready, 1)

            def queries_inverse(g):
                dve.wait_ge(eq_ready, g + 1)
                chain.link(nc.vector.tensor_reduce(qsum[:, g % 2], eq[:, g % 2], AX.X, ALU.add))
                nc.vector.reciprocal(qinv[:, g % 2], qsum[:, g % 2]).then_inc(qinv_ready, 1)

            def attended(g):
                dve.wait_ge(att_ps, g + 1)
                dve.wait_ge(qinv_ready, g + 1)
                nc.vector.tensor_tensor(att[:, :, g * HD:(g + 1) * HD].rearrange("a (j r) d -> a j r d", r=R),
                                        ps[:, B_ATT, :].rearrange("c (h r d) -> c h r d", h=NH, r=R),
                                        qinv[:, g % 2].unsqueeze(2).unsqueeze(3).to_broadcast([P, NH, R, HD]),
                                        ALU.mult).then_inc(att_ready, 1)

            dve.wait_ge(posb_ready, 1)
            for s in STEPS:
                at_block(queries_max, s)
                at_block(keys_max_of_h, s)
                at_block(keys_inverse, s - 1)
                at_block(queries_minus_max, s)
                at_block(keys_max, s)
                at_block(embed, s + 2)
                at_block(keys_minus_max, s)
                at_block(attended, s - 1)
                at_block(variance, s + 2)
                at_block(queries_inverse, s)
                if s == -2:
                    dve.wait_ge(bias_rounded, 2)
                    nc.vector.scalar_tensor_tensor(out=bias_rows[:], in0=bias_round[:].bitcast(F32),
                                                   scalar=bias_coef[:, 1:2], in1=bias_part[:],
                                                   op0=ALU.mult, op1=ALU.add).then_inc(biasr_ready, 1)
                if s == 6:
                    dve.wait_ge(rounded, 5)
                    nc.vector.tensor_copy(b2_aug[:, 0:E], b2_round[:, 0:E].bitcast(F32)).then_inc(ffn_w_ready, 1)
                    nc.vector.tensor_tensor(b2_aug[:, E:2 * E], b2_raw[:, E:2 * E], b2_round[:, E:2 * E].bitcast(F32),
                                            ALU.subtract).then_inc(ffn_w_ready, 1)
                    nc.vector.tensor_tensor(wg_hl[:, NX:2 * NX], wg_raw[:], wg_hl[:, 0:NX].bitcast(F32), ALU.subtract)\
                        .then_inc(ffn_w_ready, 1)

            def slab(u):
                return h2[:].rearrange("a j r e -> a (j r) e")[:, bass.ds(u * GT, GT), :]

            def centre(u, p):
                chain.link(nc.vector.tensor_tensor(slab(u), slab(u), att[:, bass.ds(u * GT, GT), :], ALU.add))
                dve.nop(nofuse=True)
                chain.link(nc.vector.tensor_reduce(s1b[:, p], slab(u), AX.X, ALU.add))
                nc.vector.scalar_tensor_tensor(out=xc2[:, p], in0=s1b[:, p].unsqueeze(2).to_broadcast([P, GT, E]),
                                               scalar=-1.0 / E, in1=slab(u), op0=ALU.mult, op1=ALU.add)\
                    .then_inc(xc2_ready, 1)

            def variance2(u, p):
                dve.wait_ge(sq2_ready, u + 1)
                chain.link(nc.vector.tensor_reduce(s2b[:, p], sq2[:, p], AX.X, ALU.add))
                nc.vector.tensor_scalar(var2[:, p], s2b[:, p], 1.0 / E, EPS, ALU.mult, ALU.add)\
                    .then_inc(var2_ready, 1)

            def split_tokens(u, p):
                for odd in range(2):
                    dve.wait_ge(xh_ready, 2 * u + odd + 1)
                    nc.vector.tensor_tensor(tiles(xhl[p][E:P], odd), tiles_ps(odd),
                                            tiles(xhl[p][0:E], odd).bitcast(F32), ALU.subtract).then_inc(xhl_ready, 1)

            def spread(t):
                return t.unsqueeze(2).to_broadcast([P, GT, NX])

            def top_one(scores, b, n):
                chain.link(nc.vector.tensor_reduce(best[:, 2 * n], scores[:], AX.X, ALU.max))
                chain.link(nc.vector.tensor_tensor(hit[:], scores[:], spread(best[:, 2 * n]), ALU.is_equal))
                chain.link(nc.vector.tensor_tensor(hit[:], hit[:], prio[:].unsqueeze(1).to_broadcast([P, GT, NX]),
                                                   ALU.mult))
                chain.link(nc.vector.tensor_reduce(best[:, 2 * n + 1], hit[:], AX.X, ALU.max))
                chain.link(nc.vector.tensor_tensor(pick[:, n], hit[:], spread(best[:, 2 * n + 1]), ALU.is_equal))

            def route(u, p):
                dve.wait_ge(gate_ps, u + 1)
                gates = ps[:, B_GATE, 0:GT * 2 * NX].rearrange("c (t w x) -> c t w x", t=GT, w=2)
                chain.link(nc.vector.tensor_tensor(score[:], gates[:, :, 0], bg_sb[:].unsqueeze(1)
                                                   .to_broadcast([P, GT, NX]), ALU.add))
                chain.link(nc.vector.tensor_tensor(score[:], gates[:, :, 1], score[:], ALU.add))
                top_one(score, p, 0)
                chain.link(nc.vector.scalar_tensor_tensor(out=score2[:], in0=pick[:, 0], scalar=FAR, in1=score[:],
                                                          op0=ALU.mult, op1=ALU.add))
                top_one(score2, p, 1)
                chain.link(nc.vector.tensor_tensor(mask[:, p, :, NX:2 * NX], pick[:, 0], pick[:, 1], ALU.add))
                nc.vector.tensor_scalar(mask[:, p, :, 0:NX], mask[:, p, :, NX:2 * NX], -1.0, 1.0, ALU.mult, ALU.add)\
                    .then_inc(mask_ready, 1)

            def experts_copy(u, p):
                dve.wait_ge(down_ps, 4 * u + 4)
                nc.vector.tensor_copy(ys[:, p], ps[:, B_DOWN, :]).then_inc(ys_ready, 1)

            def result(u, p):
                dve.wait_ge(yt_ps, u + 1)
                yt = ps[:, B_YT, :].rearrange("c (t y) -> c t y", t=GT)
                chain.link(nc.vector.tensor_tensor(osum[:], yt[:, :, 0:E], slab(u), ALU.add))
                nc.vector.tensor_tensor(o_sb[:, u, :].rearrange("a (r e) -> a r e", r=GT), yt[:, :, E:2 * E],
                                        osum[:], ALU.add).then_inc(out_ready, 1)

            def group(u, p, done=True, prep=True, norm=True):
                if prep:
                    if done:
                        dve.wait_ge(up_ps, 4 * u)
                    split_tokens(u + 1, 1 - p)
                if done:
                    experts_copy(u - 1, 1 - p)
                if prep:
                    route(u + 1, 1 - p)
                if norm:
                    centre(u + 3, 1 - p)
                if done:
                    result(u - 1, 1 - p)
                if norm:
                    variance2(u + 3, 1 - p)

            dve.wait_ge(res_in, 16)
            dve.wait_ge(att_ready, NH)
            centre(0, 0)
            variance2(0, 0)
            centre(1, 1)
            variance2(1, 1)
            split_tokens(0, 0)
            route(0, 0)
            centre(2, 0)
            variance2(2, 0)
            group(0, 0, done=False)
            base, before = chain.value, chain.links
            with dve.Fori(0, 6) as i:
                chain.value = base + i * (2 * 18)
                group(2 * i + 1, 1)
                group(2 * i + 2, 0)
                assert chain.links - before == 2 * 18
            chain.value = base + 12 * 18
            group(13, 1, norm=False)
            group(14, 0, norm=False)
            group(15, 1, prep=False, norm=False)
            experts_copy(15, 1)
            result(15, 1)

        @block.tensor
        def _(pe):
            pe.wait_ge(ld_ident, 16)
            pe.wait_ge(ld_w, 16 * 4)
            for n in range(4):
                mm = nc.tensor.transpose(ps[:, 7, n * E:(n + 1) * E],
                                         w_rows[:, n].rearrange("o a e -> o (a e)"), ident[0:E, 0:E])
            mm.then_inc(wt_ps, 1)
            for t in range(8):
                if t % 4 == 0:
                    pe.wait_ge(x_ready[t // 4], 4)
                if t == 7:
                    pe.wait_ge(wbd_ready, 2)
                for f in range(4):
                    mm = nc.tensor.transpose(ps[:, t, f * P:(f + 1) * P], x_pt[:, 4 * t + f].rearrange("m q p w -> m (q p w)"), ident[:])
                mm.then_inc(pt_ps, 1)
            pe.wait_ge(pt_act, 4)
            pe.wait_ge(pt_dve, 4)

            def embed(g):
                if g:
                    pe.wait_ge(h_ready, g)
                    if g >= 2:
                        pe.wait_ge(xnt_ready, g - 1)
                for b in range(4):
                    mm = nc.tensor.matmul(ps[:, B_EMB, :].rearrange("c (q b e) -> c b q e", q=2, b=4)[:, b],
                                          pt[:, b, g, :], w_bd[:, 0, :], start=True, stop=True)
                mm.then_inc(emb_ps, 1)

            def transpose_tokens(g):
                pe.wait_ge(xn_ready, g + 1)
                pe.wait_ge(h_ready, min(g + 2, NH))
                if g:
                    pe.wait_ge(xnt_ready, g)
                for b in range(4):
                    mm = nc.tensor.transpose(ps[:, B_EMB, b * P:(b + 1) * P], xn[:, g, b * P:(b + 1) * P], ident[:])
                mm.then_inc(xnt_ps, 1)

            def project(g, bank, n, done):
                nc.tensor.matmul(ps[:, bank, :], bias_sel[:],
                                 bias_rows[:, n - 1, :].unsqueeze(1).to_broadcast([P, R, E]),
                                 start=True, stop=False, skip_group_check=True)
                for b in range(4):
                    mm = nc.tensor.matmul(ps[:, bank, b * P:(b + 1) * P], xnt[:, g, b, :], w_bd[:, n, :],
                                          start=False, stop=(b == 3), skip_group_check=True)
                mm.then_inc(done, 1)

            def project_queries(g):
                pe.wait_ge(xnt_ready, g + 1)
                if g:
                    pe.wait_ge(qsub_done, g)
                project(g, B_Q, 1, q_ps)

            def project_keys(g):
                if g:
                    pe.wait_ge(ksub_done, g)
                project(g, B_K, 2, k_ps)

            def project_values(g):
                if g:
                    pe.wait_ge(vb_ready, g)
                project(g, B_V, 3, v_ps)

            def keys_max(g):
                pe.wait_ge(kmaxh_ready, g + 1)
                if g:
                    pe.wait_ge(kmaxb_ready, g)
                nc.tensor.transpose(ps[0:E, B_KMAX, 0:P], kmax_h[:, g % 2], ident[:]).then_inc(kmaxt_ps, 1)

            def keys_max_spread(g):
                pe.wait_ge(kdiag_ready, g + 1)
                nc.tensor.matmul(ps[:, B_KMAX, P:P + E], ones_row[:], kdiag[:], start=True, stop=True)\
                    .then_inc(kmaxb_ps, 1)

            def transpose_queries(g):
                pe.wait_ge(eq_ready, g + 1)
                if g:
                    pe.wait_ge(eqt_ready, g)
                for n in range(4):
                    mm = nc.tensor.transpose(ps[:, B_EQT, n * P:(n + 1) * P],
                                             eq[:, g % 2, 2 * n:2 * n + 2, :].rearrange("c h f -> c (h f)"), ident[:])
                mm.then_inc(eqt_ps, 1)

            def context(g):
                pe.wait_ge(ek_ready, g + 1)
                pe.wait_ge(vb_ready, g + 1)
                if g:
                    pe.wait_ge(ctx_ready, 2 * g)
                for h in range(NH):
                    for half in range(2):
                        mm = nc.tensor.matmul(ps[half * E:(half + 1) * E, B_CTX, 0:E + 1], ek[:, g % 2, h, :],
                                              vb[:, g % 2, h, :], start=(h == 0), stop=(h == NH - 1))
                mm.then_inc(ctx_ps, 1)

            def attend(g):
                pe.wait_ge(eqt_ready, g + 1)
                pe.wait_ge(ctx_ready, 2 * (g + 1))
                if g:
                    pe.wait_ge(att_ready, g)
                for n in range(4):
                    mm = nc.tensor.matmul(ps[:, B_ATT, n * P:(n + 1) * P], eqt[:, g % 2, n, :], ctx_bd[:, g % 2, :],
                                          start=True, stop=True)
                mm.then_inc(att_ps, 1)

            for s in STEPS:
                if s == 0:
                    pe.wait_ge(biasr_ready, 1)
                    pe.wait_ge(zeroed, 10)
                at_block(project_queries, s)
                at_block(project_keys, s)
                at_block(context, s - 1)
                at_block(keys_max, s)
                at_block(embed, s + 2)
                at_block(project_values, s)
                at_block(keys_max_spread, s)
                at_block(transpose_tokens, s + 1)
                at_block(attend, s - 1)
                at_block(transpose_queries, s)

            def transpose2(u, p):
                pe.wait_ge(xn2_ready, u + 1)
                pe.nop(nofuse=True)
                for t in range(2):
                    mm = nc.tensor.transpose(ps[:, B_T, t * P:(t + 1) * P],
                                             xn2[:, p, 2 * t:2 * t + 2, :].rearrange("a t e -> a (t e)"), ident[:])
                mm.then_inc(xt_ps, 1)

            def gate(u, p):
                pe.wait_ge(xhl_ready, 2 * u + 2)
                for t in range(GT):
                    mm = nc.tensor.matmul(ps[:, B_GATE, t * 2 * NX:(t + 1) * 2 * NX], xhl[p][:, t * P:(t + 1) * P],
                                          wg_hl[:], start=True, stop=True)
                mm.then_inc(gate_ps, 1)

            def transpose_mask(u, p):
                pe.wait_ge(mask_ready, u + 1)
                nc.tensor.transpose(ps[:, B_GATE, 0:P], mask[:, p].rearrange("a t m -> a (t m)"), ident[:])\
                    .then_inc(mask_ps, 1)

            def up(u, p, pair, wait_bank=True):
                if wait_bank:
                    pe.wait_ge(hid_ready, 4 * u + pair - 1)
                for k in range(2):
                    e = 2 * pair + k
                    bank = 2 * (pair % 2) + k
                    nc.tensor.matmul(ps[:, bank, :], w1_hh[:, e, :], xhl[p][:], start=True, stop=False)
                    mm = nc.tensor.matmul(ps[:, bank, :], w_aug[:, e * HID:(e + 1) * HID], xm[p][:],
                                          start=False, stop=True)
                mm.then_inc(up_ps, 1)

            def down(u, pair):
                pe.wait_ge(hid_ready, 4 * u + pair + 1)
                for k in range(2):
                    mm = nc.tensor.matmul(ps[k * E:(k + 1) * E, B_DOWN, :], w2_sb[:, 2 * pair + k, :],
                                          hid[:, pair % 2, k, :], start=False, stop=(pair == 3),
                                          skip_group_check=True)
                mm.then_inc(down_ps, 1)

            def down_bias(u, p):
                nc.tensor.matmul(ps[:, B_DOWN, :], b2_aug[:], xm[p][:], start=True, stop=False,
                                 skip_group_check=True)

            def transpose_result(u, p):
                pe.wait_ge(ys_ready, u + 1)
                for t in range(GT):
                    mm = nc.tensor.transpose(ps[:, B_YT, t * P:(t + 1) * P], ys[:, p, t * P:(t + 1) * P], ident[:])
                mm.then_inc(yt_ps, 1)

            def group(u, p, first=False, prep=True):
                if prep:
                    pe.wait_ge(xhl_ready, 2 * u + 2)
                    transpose2(u + 1, 1 - p)
                pe.wait_ge(xmx_ready, u + 1)
                pe.wait_ge(xmm_ready, u + 1)
                up(u, p, 0, not first)
                if not first:
                    down(u - 1, 3)
                if prep:
                    gate(u + 1, 1 - p)
                up(u, p, 1, not first)
                if not first:
                    pe.wait_ge(ys_ready, u)
                down_bias(u, p)
                down(u, 0)
                up(u, p, 2)
                down(u, 1)
                if not first:
                    transpose_result(u - 1, 1 - p)
                if prep:
                    transpose_mask(u + 1, 1 - p)
                up(u, p, 3)
                down(u, 2)

            pe.wait_ge(att_ready, NH)
            pe.wait_ge(ffn_w_ready, 4)
            transpose2(0, 0)
            gate(0, 0)
            transpose_mask(0, 0)
            group(0, 0, first=True)
            with pe.Fori(0, 6) as i:
                group(2 * i + 1, 1)
                group(2 * i + 2, 0)
            group(13, 1)
            group(14, 0)
            group(15, 1, prep=False)
            down(15, 3)
            transpose_result(15, 1)


_INS = ['x', 'L0_tok_W', 'L0_tok_b', 'L0_tok_pos_embed', 'L0_attn_Wq', 'L0_attn_bq', 'L0_attn_Wk', 'L0_attn_bk',
        'L0_attn_Wv', 'L0_attn_bv', 'L0_ffn_Wg', 'L0_ffn_bg', 'L0_ffn_W1', 'L0_ffn_b1', 'L0_ffn_W2', 'L0_ffn_b2']


def _constants(np):
    rows = np.zeros((16, NX, HID), np.float32)
    for e in range(NX):
        rows[e, e, :] = -BIG
    coef = np.zeros((KM, 2), np.float32)
    coef[0:E] = (1.0, -1.0)
    coef[E:E + 16] = (1.0, 0.0)
    coef[E + 16] = (0.0, 1.0)
    coef[E + 17] = (1.0, -1.0)
    prio = np.tile(np.arange(NX, 0, -1, dtype=np.float32), (P, 1))
    bias = np.zeros((P, 2), np.float32)
    bias[0] = (0.0, 1.0)
    bias[1] = (1.0, -1.0)
    return {"ident": np.eye(P, dtype=np.float32), "rows": rows.reshape(16, NX * HID), "coef": coef, "prio": prio, "bias": bias}


def kernel(**inputs):
    import numpy as _np
    import concourse.bacc as _bacc
    from concourse import mybir as _mybir
    from concourse.bass_utils import run_bass_kernel_spmd as _run

    nc = _bacc.Bacc("TRN2", target_bir_lowering=False, num_devices=1)
    arrays, args = {}, []
    for name in _INS:
        a = _np.ascontiguousarray(inputs[name])
        arrays[f"in_{name}_dram"] = a
        args.append(nc.dram_tensor(f"in_{name}_dram", a.shape, _mybir.dt.from_np(a.dtype), kind="ExternalInput").ap())
    for name, a in _constants(_np).items():
        arrays[f"const_{name}_dram"] = a
        args.append(nc.dram_tensor(f"const_{name}_dram", a.shape, _mybir.dt.from_np(a.dtype), kind="ExternalInput").ap())
    args.append(nc.dram_tensor("out_0_dram", (R, C, E), _mybir.dt.float32, kind="ExternalOutput").ap())
    bass_vit_layer_kernel(nc, *args)
    r = _run(nc, [arrays], core_ids=[0])
    return r.results[0]["out_0_dram"]
```

```python
from contextlib import ExitStack

import concourse.bass as bass
from concourse import mybir

F32 = mybir.dt.float32
F32R = mybir.dt.float32r
ALU = mybir.AluOpType
ACT = mybir.ActivationFunctionType
AX = mybir.AxisListType

P = 128
R = 8
C = 1024
E = 64
NH = 8
HD = E // NH
PATCH = 8
ROW = R * E
NX = 8
HID = 128
NG = 16
GT = 4
GW = GT * E
NM = 18
KM = E + NM
EPS = 1e-5
BIG = float(2 ** 100)
FAR = -3.0e38


class Chain:

    def __init__(self, eng, sem):
        self.eng, self.sem, self.value, self.links = eng, sem, 0, 0

    def link(self, ins):
        self.value = self.value + 1
        self.links += 1
        ins.then_inc(self.sem, 1)
        self.eng.wait_ge(self.sem, self.value)


def bass_vit_layer_kernel(nc, x, tok_w, tok_b, pos, wq, bq, wk, bk, wv, bv, wg, bg, w1, b1, w2, b2,
                          c_ident, c_rows, c_coef, c_prio, c_bias, out):
    h_dram = nc.dram_tensor("residual_by_patch", (C, ROW), F32, kind="Internal").ap()

    with ExitStack() as ctx:
        def sb(name, shape, dt=F32):
            return ctx.enter_context(nc.sbuf_tensor(name, shape, dt))

        def sem(name):
            return ctx.enter_context(nc.semaphore(name))

        ident = sb("ident", [P, P])
        w_rows = sb("w_rows", [E, 4, 2, E])
        w_bd = sb("w_bd", [P, 4, P])
        tokb_sb = sb("tokb_sb", [P, E])
        ones_row = sb("ones_row", [E, P])
        bias_raw = sb("bias_raw", [P, 2, E])
        bias_round = sb("bias_round", [P, 2, E], F32R)
        bias_part = sb("bias_part", [P, 2, E])
        bias_rows = sb("bias_rows", [P, 2, E], F32R)
        bv_sb = sb("bv_sb", [P, NH, HD])
        bias_coef = sb("bias_coef", [P, 2])
        bias_sel = sb("bias_sel", [P, P], F32R)
        minus_half = sb("minus_half", [P, 8])
        gelu_first = sb("gelu_first", [P, 8])
        w1_raw = sb("w1_raw", [P, NX, HID])
        w1_hh = sb("w1_hh", [P, NX, HID], F32R)
        aug_raw = sb("aug_raw", [KM, NX * HID])
        aug_round = sb("aug_round", [KM, NX * HID], F32R)
        aug_part = sb("aug_part", [KM, NX * HID])
        w_aug = sb("w_aug", [KM, NX * HID], F32R)
        coef = sb("coef", [KM, 2])
        b2_raw = sb("b2_raw", [KM, 2 * E])
        b2_round = sb("b2_round", [KM, 2 * E], F32R)
        b2_aug = sb("b2_aug", [KM, 2 * E], F32R)
        w2_sb = sb("w2_sb", [HID, NX, E])
        wg_raw = sb("wg_raw", [P, NX])
        wg_hl = sb("wg_hl", [P, 2 * NX], F32R)
        bg_sb = sb("bg_sb", [P, NX])
        prio = sb("prio", [P, NX])

        x_sb = sb("x_sb", [P, 2, PATCH, 32, PATCH])
        x_pt = sb("x_pt", [P, 32, 2, PATCH, PATCH])
        pt = sb("pt", [P, 4, NH, P])
        posb = sb("posb", [P, NH, E])
        h_sb = sb("h_sb", [P, NH, ROW])
        xc = sb("xc", [P, NH, ROW])
        sq = x_sb[:].rearrange("p q k f w -> p (q k f w)").rearrange("p (g f) -> p g f", g=NH)
        s1 = sb("s1", [P, NH, R])
        mean = sb("mean", [P, NH, R])
        s2 = sb("s2", [P, NH, R])
        var = sb("var", [P, NH, R])
        rstd = sb("rstd", [P, NH, R])

        xn = xc
        xnt = x_pt[:].rearrange("p f q k w -> p (f q k w)").rearrange("p (g b c) -> p g b c", g=NH, b=4)
        kmax_h = sb("kmax_h", [P, 2, E])
        kmax = sb("kmax", [E, 2])
        kdiag = sb("kdiag", [E, E])
        kmax_all = sb("kmax_all", [P, E])
        kb = sb("kb", [P, 2, R, NH, HD])
        qb = sb("qb", [P, 2, R, NH, HD])
        eq = sb("eq", [P, 2, NH, E])
        ek = sb("ek", [P, 2, NH, E])
        vb = sb("vb", [P, 2, NH, E + 1])
        qmax = sb("qmax", [P, 2, NH])
        qsum = sb("qsum", [P, 2, NH])
        qinv = sb("qinv", [P, 2, NH])
        kinv = sb("kinv", [P, 2])
        ctx_bd = sb("ctx_bd", [P, 2, P])
        eqt = sb("eqt", [P, 2, 4, P])
        att = sb("att", [P, NH * R, E])
        h2 = sb("h2", [P, NH, R, E])

        xc2 = sb("xc2", [P, 2, GT, E])
        sq2 = sb("sq2", [P, 2, GT, E])
        s1b = sb("s1b", [P, 2, GT])
        s2b = sb("s2b", [P, 2, GT])
        var2 = sb("var2", [P, 2, GT])
        rstd2 = sb("rstd2", [P, 2, GT])
        xn2 = sb("xn2", [P, 2, GT, E])
        xhl = [sb(f"xhl{n}", [P, 512], F32R) for n in range(2)]
        xm = [sb(f"xm{n}", [KM, 512], F32R) for n in range(2)]
        score = sb("score", [P, GT, NX])
        score2 = sb("score2", [P, GT, NX])
        hit = sb("hit", [P, GT, NX])
        pick = sb("pick", [P, 2, GT, NX])
        best = sb("best", [P, 4, GT])
        mask = sb("mask", [P, 2, GT, 32])
        hid = sb("hid", [HID, 2, 2, 512])
        aug_minus = hid[0:KM].rearrange("k a b c -> k (a b c)")[:, 0:NX * HID]
        ys = sb("ys", [P, 2, 512])
        osum = sb("osum", [P, GT, E])
        o_sb = xc[:].rearrange("p g (t f) -> p (g t) f", t=2)

        ps = ctx.enter_context(nc.psum_tensor("ps", [P, 8, 512], F32))

        ld_ident, ld_w, ld_bias = sem("ld_ident"), sem("ld_w"), sem("ld_bias")
        ld_x = [[sem(f"ld_x{part}_{n}") for n in range(4)] for part in range(2)]
        x_ready = [sem("x_ready_left"), sem("x_ready_right")]
        ld_ffn, ld_qkb, ld_bv = sem("ld_ffn"), sem("ld_qkb"), sem("ld_bv")
        res_out, res_in = sem("res_out"), sem("res_in")
        stored = [sem("stored_even"), sem("stored_odd")]
        zeroed, wt_ps, wbd_ready, posb_ready = sem("zeroed"), sem("wt_ps"), sem("wbd_ready"), sem("posb_ready")
        pt_ps, pt_act, pt_dve = sem("pt_ps"), sem("pt_act"), sem("pt_dve")
        rounded, ffn_w_ready, biasr_ready = sem("rounded"), sem("ffn_w_ready"), sem("biasr_ready")
        bias_rounded = sem("bias_rounded")
        emb_ps, h_ready, xc_ready, sq_ready = sem("emb_ps"), sem("h_ready"), sem("xc_ready"), sem("sq_ready")
        s1_ready, s2_ready, kmax_ready, qsum_ready = sem("s1_ready"), sem("s2_ready"), sem("kmax_ready"), sem("qsum_ready")
        mean_ready, var_ready, rstd_ready = sem("mean_ready"), sem("var_ready"), sem("rstd_ready")
        xn_ready, xnt_ps, xnt_ready = sem("xn_ready"), sem("xnt_ps"), sem("xnt_ready")
        q_ps, qmax_ready, qsub_done, eq_ready = sem("q_ps"), sem("qmax_ready"), sem("qsub_done"), sem("eq_ready")
        eqt_ps, eqt_ready, qinv_ready = sem("eqt_ps"), sem("eqt_ready"), sem("qinv_ready")
        k_ps, kmaxh_ready, kmaxt_ps, kdiag_ready = sem("k_ps"), sem("kmaxh_ready"), sem("kmaxt_ps"), sem("kdiag_ready")
        kmaxb_ps, kmaxb_ready, ksub_done, ek_ready = sem("kmaxb_ps"), sem("kmaxb_ready"), sem("ksub_done"), sem("ek_ready")
        vbias_ready = sem("vbias_ready")
        v_ps, vb_ready, ctx_ps = sem("v_ps"), sem("vb_ready"), sem("ctx_ps")
        kinv_ready, ctx_ready = sem("kinv_ready"), sem("ctx_ready")
        att_ps, att_ready = sem("att_ps"), sem("att_ready")
        xc2_ready, sq2_ready = sem("xc2_ready"), sem("sq2_ready")
        var2_ready, rstd2_ready = sem("var2_ready"), sem("rstd2_ready")
        xn2_ready, xt_ps, xh_ready, xmx_ready = sem("xn2_ready"), sem("xt_ps"), sem("xh_ready"), sem("xmx_ready")
        xhl_ready, gate_ps, mask_ready = sem("xhl_ready"), sem("gate_ps"), sem("mask_ready")
        mask_ps, xmm_ready = sem("mask_ps"), sem("xmm_ready")
        up_ps, hid_ready, down_ps = sem("up_ps"), sem("hid_ready"), sem("down_ps")
        ys_ready, yt_ps, out_ready = sem("ys_ready"), sem("yt_ps"), sem("out_ready")
        dve_chain = sem("dve_chain")

        block = ctx.enter_context(nc.Block())

        STEPS = range(-2, NH - 1)
        LAST = NH - 1

        def at_block(stage, g):
            if 0 <= g < NH:
                stage(g)

        B_EMB, B_K, B_Q, B_V, B_KMAX, B_CTX, B_EQT, B_ATT = range(8)
        B_DOWN, B_T, B_GATE, B_YT = 4, 5, 6, 7

        def tiles(t, odd):
            return t.rearrange("k (t o c) -> k o t c", o=2, c=P)[:, odd]

        def tiles_ps(odd):
            return ps[odd * E:(odd + 1) * E, B_T, 0:2 * P].rearrange("k (t c) -> k t c", t=2)

        def load_x(eng, fh):
            images = x.rearrange("(q b) o (m p) c -> q (b o m) p c", q=2, p=PATCH)
            for part in range(2):
                for q in range(2):
                    at = fh * 256 + part * 128
                    eng.dma_start(x_sb[fh * 64:(fh + 1) * 64, q, :, part * 16:(part + 1) * 16, :]
                                  .rearrange("m p f w -> m p (f w)"),
                                  images[q, :, :, at:at + 128]).then_inc(ld_x[part][2 * fh + q], 16)

        def regroup_x(eng, copy, part, fh, q):
            at, f = slice(fh * 64, (fh + 1) * 64), slice(part * 16, (part + 1) * 16)
            eng.wait_ge(ld_x[part][2 * fh + q], 16)
            copy(x_pt[at, f, q].rearrange("m f p w -> m p f w"), x_sb[at, q, :, f]).then_inc(x_ready[part], 1)

        def patches_out(t):
            return (pt[:].rearrange("k b g (m a f) -> k f a (b g m)", m=2, a=2)[:, 4 * t:4 * t + 4],
                    ps[:, t, :].rearrange("k (f a c) -> k f a c", f=4, a=2))

        @block.sync
        def _(sp):
            sp.dma_start(ident[:], c_ident).then_inc(ld_ident, 16)
            load_x(sp, 0)
            sp.dma_start(tokb_sb[:], tok_b.partition_broadcast(P)).then_inc(ld_bias, 16)
            sp.dma_start(posb[:], pos[0].rearrange("(g c) e -> c g e", g=NH)).then_inc(ld_bias, 16)
            sp.wait_ge(zeroed, 2)
            for n, b in enumerate((bq, bk)):
                for row in range(2):
                    sp.dma_start(bias_raw[row:row + 1, n, :], b.rearrange("(a e) -> a e", a=1)).then_inc(ld_qkb, 16)
            sp.dma_start(bias_coef[:], c_bias).then_inc(ld_qkb, 16)
            sp.dma_start(bv_sb[:].rearrange("c h d -> c (h d)"), bv.partition_broadcast(P)).then_inc(ld_bv, 16)
            w1_in = w1.rearrange("x d h -> d x h")
            for half in range(2):
                sp.dma_start(w1_raw[half * E:(half + 1) * E], w1_in).then_inc(ld_ffn, 16)
            sp.dma_start(aug_raw[0:E].rearrange("d (x h) -> d x h", x=NX), w1_in).then_inc(ld_ffn, 16)
            sp.dma_start(aug_raw[E:E + 16], c_rows).then_inc(ld_ffn, 16)
            for n in range(2):
                sp.dma_start(aug_raw[E + 16 + n:E + 17 + n],
                             b1.rearrange("(a x) h -> a (x h)", a=1)).then_inc(ld_ffn, 16)
            for n in range(2):
                sp.dma_start(b2_raw[E + 8:E + 16, n * E:(n + 1) * E], b2).then_inc(ld_ffn, 16)
            sp.dma_start(coef[:], c_coef).then_inc(ld_ffn, 16)
            sp.dma_start(w2_sb[:], w2.rearrange("x h d -> h x d")).then_inc(ld_ffn, 16)
            for half in range(2):
                sp.dma_start(wg_raw[half * E:(half + 1) * E], wg).then_inc(ld_ffn, 16)
            sp.dma_start(bg_sb[:], bg.partition_broadcast(P)).then_inc(ld_ffn, 16)
            sp.dma_start(prio[:], c_prio).then_inc(ld_ffn, 16)
            res_rows = h_dram.rearrange("(g c) f -> g c f", g=NH)
            with sp.Fori(0, NH) as g:
                sp.wait_ge(h_ready, g + 1)
                sp.dma_start(res_rows[g], h_sb[:, g, :]).then_inc(res_out, 16)
            sp.wait_ge(res_out, 16 * NH)
            sp.dma_start(h2[:].rearrange("a j r e -> a (j r e)"),
                         h_dram.rearrange("(a j) f -> a (j f)", j=8)).then_inc(res_in, 16)
            out_v = out.rearrange("r (a j) e -> j a r e", j=8)
            with sp.Fori(0, NG // 2) as j:
                for half in range(2):
                    sp.wait_ge(out_ready, 2 * j + half + 1)
                    sp.dma_start(out_v[j, :, GT * half:GT * (half + 1), :],
                                 o_sb[:, 2 * j + half, :].rearrange("a (r e) -> a r e", r=GT)).then_inc(stored[half], 16)
            for half in range(2):
                sp.wait_ge(stored[half], 16 * (NG // 2))

        @block.gpsimd
        def _(pool):
            for n, w in enumerate((tok_w, wq, wk, wv)):
                pool.dma_start(w_rows[:, n], w.unsqueeze(1).to_broadcast([E, 2, E])).then_inc(ld_w, 16)
            nc.gpsimd.memset(bias_raw[:], 0.0).then_inc(zeroed, 1)
            nc.gpsimd.memset(b2_raw[:], 0.0).then_inc(zeroed, 1)
            nc.gpsimd.memset(w_bd[:], 0.0).then_inc(zeroed, 1)
            nc.gpsimd.memset(minus_half[:], -0.5).then_inc(zeroed, 1)
            pool.wait_ge(zeroed, 4)
            nc.gpsimd.memset(ctx_bd[:], 0.0).then_inc(zeroed, 1)
            nc.gpsimd.memset(ones_row[:], 1.0).then_inc(zeroed, 1)
            nc.gpsimd.memset(vb[:], float(HD) ** -1.0).then_inc(zeroed, 1)
            nc.gpsimd.memset(mask[:], 1.0).then_inc(zeroed, 1)
            nc.gpsimd.memset(bias_sel[:].bitcast(F32), 0.0).then_inc(zeroed, 1)
            pool.wait_ge(zeroed, 9)
            nc.gpsimd.memset(bias_sel[0:2, :].bitcast(F32), 1.0).then_inc(zeroed, 1)
            pool.wait_ge(zeroed, 10)
            pool.wait_ge(ld_bias, 16 * 2)
            nc.gpsimd.tensor_tensor(posb[:], posb[:], tokb_sb[:].unsqueeze(1).to_broadcast([P, NH, E]),
                                    ALU.add).then_inc(posb_ready, 1)
            def centre1(g):
                if g >= 2:
                    pool.wait_ge(mean_ready, g - 1)
                    nc.gpsimd.tensor_tensor(xc[:, g, :].rearrange("c (r e) -> c r e", r=R),
                                            h_sb[:, g, :].rearrange("c (r e) -> c r e", r=R),
                                            mean[:, g, :].unsqueeze(2).to_broadcast([P, R, E]), ALU.subtract)\
                        .then_inc(xc_ready, 1)

            def values_bias(g):
                pool.wait_ge(vb_ready, g + 1)
                if g == 0:
                    pool.wait_ge(ld_bv, 16)
                values = vb[:, g % 2, :, 0:E].rearrange("c h (r d) -> c h r d", r=R)
                nc.gpsimd.tensor_tensor(values, values, bv_sb[:].unsqueeze(2).to_broadcast([P, NH, R, HD]), ALU.add)\
                    .then_inc(vbias_ready, 1)

            def normalise1(g):
                pool.wait_ge(var_ready, g + 1)
                nc.gpsimd.tensor_tensor(rstd[:, g, :], var[:, g, :], minus_half[:], ALU.pow).then_inc(rstd_ready, 1)
                pool.wait_ge(rstd_ready, g + 1)
                nc.gpsimd.tensor_tensor(xn[:, g, :].rearrange("c (r e) -> c r e", r=R),
                                        xc[:, g, :].rearrange("c (r e) -> c r e", r=R),
                                        rstd[:, g, :].unsqueeze(2).to_broadcast([P, R, E]), ALU.mult)\
                    .then_inc(xn_ready, 1)

            for s in STEPS:
                at_block(centre1, s + 2)
                at_block(values_bias, s)
                at_block(normalise1, s + 2)
            values_bias(LAST)
            pool.wait_ge(rounded, 6)
            nc.gpsimd.tensor_tensor(w_aug[:], aug_part[:], aug_minus, ALU.add).then_inc(ffn_w_ready, 1)

            def norm2(u, p, first=False):
                pool.wait_ge(var2_ready, u + 1)
                nc.gpsimd.tensor_tensor(rstd2[:, p], var2[:, p], minus_half[:, 0:GT], ALU.pow)\
                    .then_inc(rstd2_ready, 1)
                pool.wait_ge(rstd2_ready, u + 1)
                if not first:
                    pool.wait_ge(xt_ps, u - 1)
                nc.gpsimd.tensor_tensor(xn2[:, p], xc2[:, p],
                                        rstd2[:, p].unsqueeze(2).to_broadcast([P, GT, E]), ALU.mult)\
                    .then_inc(xn2_ready, 1)

            def tokens_again(u, p):
                pool.wait_ge(xh_ready, 2 * u + 2)
                pool.nop(nofuse=True)
                nc.gpsimd.tensor_copy(xm[p][0:E], xhl[p][0:E].bitcast(F32)).then_inc(xmx_ready, 1)

            def group(u, p):
                pool.wait_ge(up_ps, 4 * u)
                tokens_again(u + 1, 1 - p)
                norm2(u + 3, 1 - p)

            norm2(0, 0, first=True)
            norm2(1, 1, first=True)
            tokens_again(0, 0)
            norm2(2, 0)
            tokens_again(1, 1)
            norm2(3, 1)
            with pool.Fori(0, 6) as i:
                group(2 * i + 1, 1)
                group(2 * i + 2, 0)
            for u in (13, 14):
                pool.wait_ge(up_ps, 4 * u)
                tokens_again(u + 1, (u + 1) % 2)

        @block.scalar
        def _(act):
            load_x(act, 1)
            for t in range(1, 8, 2):
                act.wait_ge(pt_ps, t + 1)
                dst, src = patches_out(t)
                nc.scalar.activation(dst, src, ACT.Copy).then_inc(pt_act, 1)
            act.wait_ge(ld_qkb, 16 * 5)
            nc.scalar.activation(bias_round[:], bias_raw[:], ACT.Copy).then_inc(bias_rounded, 1)
            nc.scalar.activation(bias_part[:], bias_raw[:], ACT.Copy, scale=bias_coef[:, 0:1]).then_inc(bias_rounded, 1)

            def squares1(g):
                act.wait_ge(xc_ready, g + 1)
                nc.scalar.activation(sq[:, g, :], xc[:, g, :], ACT.Square).then_inc(sq_ready, 1)

            def tokens1(g):
                act.wait_ge(xnt_ps, g + 1)
                nc.scalar.activation(xnt[:, g].rearrange("k b c -> k (b c)"), ps[:, B_EMB, :], ACT.Copy)\
                    .then_inc(xnt_ready, 1)

            def exp_queries(g):
                act.wait_ge(qsub_done, g + 1)
                nc.scalar.activation(eq[:, g % 2].rearrange("c h (r d) -> c r h d", r=R), qb[:, g % 2], ACT.Exp)\
                    .then_inc(eq_ready, 1)

            def keys_max_copy(g):
                act.wait_ge(kmaxb_ps, g + 1)
                nc.scalar.activation(kmax_all[:], ps[:, B_KMAX, P:P + E], ACT.Copy).then_inc(kmaxb_ready, 1)

            def values(g):
                act.wait_ge(v_ps, g + 1)
                nc.scalar.activation(vb[:, g % 2, :, 0:E].rearrange("c h (r d) -> c r h d", r=R),
                                     ps[:, B_V, :].rearrange("c (r h d) -> c r h d", r=R, h=NH), ACT.Copy)\
                    .then_inc(vb_ready, 1)

            def exp_keys(g):
                act.wait_ge(ksub_done, g + 1)
                nc.scalar.activation(ek[:, g % 2].rearrange("c h (r d) -> c r h d", r=R), kb[:, g % 2], ACT.Exp)\
                    .then_inc(ek_ready, 1)

            def context_scaled(g):
                act.wait_ge(kinv_ready, g + 1)
                for half in (slice(0, E), slice(E, P)):
                    nc.scalar.activation(ctx_bd[half, g % 2, half], ps[half, B_CTX, 0:E], ACT.Copy,
                                         scale=kinv[half, g % 2:g % 2 + 1]).then_inc(ctx_ready, 1)

            def queries_copy(g):
                act.wait_ge(eqt_ps, g + 1)
                nc.scalar.activation(eqt[:, g % 2].rearrange("k b c -> k (b c)"), ps[:, B_EQT, :], ACT.Copy)\
                    .then_inc(eqt_ready, 1)

            for s in STEPS:
                at_block(context_scaled, s - 1)
                at_block(exp_queries, s)
                at_block(keys_max_copy, s)
                at_block(values, s)
                at_block(tokens1, s + 1)
                at_block(squares1, s + 2)
                at_block(exp_keys, s)
                at_block(queries_copy, s)
                if s == 3:
                    act.wait_ge(ld_ffn, 16 * 14)
                    nc.scalar.activation(w1_hh[:], w1_raw[:], ACT.Copy).then_inc(rounded, 1)
                    nc.scalar.activation(aug_round[:], aug_raw[:], ACT.Copy).then_inc(rounded, 1)
                if s == 4:
                    nc.scalar.activation(aug_part[:], aug_raw[:], ACT.Copy, scale=coef[:, 0:1]).then_inc(rounded, 1)
                    nc.scalar.activation(b2_round[:], b2_raw[:], ACT.Copy).then_inc(rounded, 1)
                    nc.scalar.activation(wg_hl[:, 0:NX], wg_raw[:], ACT.Copy).then_inc(rounded, 1)
                    act.wait_ge(rounded, 2)
                    nc.scalar.activation(aug_minus, aug_round[:].bitcast(F32), ACT.Copy, scale=coef[:, 1:2])\
                        .then_inc(rounded, 1)

            keys_max_copy(LAST)
            values(LAST)
            exp_queries(LAST)
            exp_keys(LAST)
            context_scaled(LAST - 1)
            queries_copy(LAST)
            context_scaled(LAST)

            def squares(u, p):
                act.wait_ge(xc2_ready, u + 1)
                nc.scalar.activation(sq2[:, p], xc2[:, p], ACT.Square).then_inc(sq2_ready, 1)

            def tokens_high(u, p):
                act.wait_ge(xt_ps, u + 1)
                for odd in range(2):
                    nc.scalar.activation(tiles(xhl[p][0:E], odd), tiles_ps(odd), ACT.Copy).then_inc(xh_ready, 1)

            def mask_copy(u, p):
                act.wait_ge(mask_ps, u + 1)
                for t in range(GT):
                    ins = nc.scalar.activation(xm[p][E:KM, t * P:(t + 1) * P], ps[32 * t:32 * t + NM, B_GATE, 0:P],
                                               ACT.Copy)
                ins.then_inc(xmm_ready, 1)

            def gelu(u, pair, wait_hid=True):
                act.wait_ge(up_ps, 4 * u + pair + 1)
                if wait_hid:
                    act.wait_ge(down_ps, 4 * u + pair - 1)
                at = 2 * (pair % 2)
                nc.scalar.activation(hid[:, pair % 2], ps[:, at:at + 2, :], ACT.Gelu).then_inc(hid_ready, 1)

            def group(u, p, first=False, prep=True, norm=True):
                if prep and not first:
                    act.wait_ge(up_ps, 4 * u)
                    tokens_high(u + 1, 1 - p)
                gelu(u, 0, not first)
                gelu(u, 1, not first)
                gelu(u, 2)
                if prep:
                    mask_copy(u + 1, 1 - p)
                if norm:
                    squares(u + 3, 1 - p)
                gelu(u, 3)

            nc.scalar.activation(gelu_first[:], minus_half[:], ACT.Gelu)
            squares(0, 0)
            squares(1, 1)
            tokens_high(0, 0)
            tokens_high(1, 1)
            mask_copy(0, 0)
            squares(2, 0)
            group(0, 0, first=True)
            with act.Fori(0, 6) as i:
                group(2 * i + 1, 1)
                group(2 * i + 2, 0)
            group(13, 1, norm=False)
            group(14, 0, norm=False)
            group(15, 1, prep=False, norm=False)

        @block.vector
        def _(dve):
            chain = Chain(dve, dve_chain)
            for part in range(2):
                for q in range(2):
                    for fh in (1, 0):
                        regroup_x(dve, nc.vector.tensor_copy, part, fh, q)
            dve.wait_ge(zeroed, 4)
            dve.wait_ge(wt_ps, 1)
            wt = ps[:, 7, 0:4 * E].rearrange("k (w e) -> k w e", w=4)
            nc.vector.tensor_copy(w_bd[0:E, :, 0:E], wt[0:E]).then_inc(wbd_ready, 1)
            nc.vector.tensor_copy(w_bd[E:P, :, E:P], wt[E:P]).then_inc(wbd_ready, 1)
            for t in range(0, 8, 2):
                dve.wait_ge(pt_ps, t + 1)
                dst, src = patches_out(t)
                nc.vector.tensor_copy(dst, src).then_inc(pt_dve, 1)

            def rows(t, g):
                return t[:, g, :].rearrange("c (r e) -> c r e", r=R)

            def embed(g):
                dve.wait_ge(emb_ps, g + 1)
                nc.vector.tensor_tensor(rows(h_sb, g), rows(ps, B_EMB),
                                        posb[:, g, :].unsqueeze(1).to_broadcast([P, R, E]), ALU.add)\
                    .then_inc(h_ready, 1)

            def sum1(g):
                dve.wait_ge(h_ready, g + 1)
                nc.vector.tensor_reduce(s1[:, g, :], rows(h_sb, g), AX.X, ALU.add).then_inc(s1_ready, 1)

            def mean1(g):
                dve.wait_ge(s1_ready, g + 1)
                if g < 2:
                    nc.vector.scalar_tensor_tensor(out=rows(xc, g), in0=s1[:, g, :].unsqueeze(2).to_broadcast([P, R, E]),
                                                   scalar=-1.0 / E, in1=rows(h_sb, g), op0=ALU.mult, op1=ALU.add)\
                        .then_inc(xc_ready, 1)
                else:
                    nc.vector.tensor_scalar(mean[:, g, :], s1[:, g, :], 1.0 / E, None, ALU.mult)\
                        .then_inc(mean_ready, 1)

            def squares_sum(g):
                dve.wait_ge(sq_ready, g + 1)
                nc.vector.tensor_reduce(s2[:, g, :], rows(sq, g), AX.X, ALU.add).then_inc(s2_ready, 1)

            def variance(g):
                dve.wait_ge(s2_ready, g + 1)
                nc.vector.tensor_scalar(var[:, g, :], s2[:, g, :], 1.0 / E, EPS, ALU.mult, ALU.add)\
                    .then_inc(var_ready, 1)

            def bank(b):
                return ps[:, b, :].rearrange("c (r h d) -> c r h d", r=R, h=NH)

            def queries_max(g):
                dve.wait_ge(q_ps, g + 1)
                nc.vector.tensor_reduce(qmax[:, g % 2], bank(B_Q).rearrange("c r h d -> c h r d"), AX.XY, ALU.max)\
                    .then_inc(qmax_ready, 1)

            def queries_minus_max(g):
                dve.wait_ge(qmax_ready, g + 1)
                nc.vector.tensor_tensor(qb[:, g % 2], bank(B_Q),
                                        qmax[:, g % 2].unsqueeze(1).unsqueeze(3).to_broadcast([P, R, NH, HD]),
                                        ALU.subtract).then_inc(qsub_done, 1)

            def keys_max_of_h(g):
                dve.wait_ge(k_ps, g + 1)
                nc.vector.tensor_reduce(kmax_h[:, g % 2].rearrange("c (r d) -> c r d", r=R),
                                        bank(B_K).rearrange("c r h d -> c r d h"), AX.X, ALU.max)\
                    .then_inc(kmaxh_ready, 1)

            def keys_max(g):
                dve.wait_ge(kmaxt_ps, g + 1)
                nc.vector.tensor_reduce(kmax[:, g % 2:g % 2 + 1], ps[0:E, B_KMAX, 0:P], AX.X, ALU.max)\
                    .then_inc(kmax_ready, 1)

            def keys_diagonal(g):
                dve.wait_ge(kmax_ready, g + 1)
                nc.vector.tensor_scalar(kdiag[:], ident[0:E, 0:E], kmax[:, g % 2:g % 2 + 1], None, ALU.mult)\
                    .then_inc(kdiag_ready, 1)

            def keys_minus_max(g):
                dve.wait_ge(kmaxb_ready, g + 1)
                nc.vector.tensor_tensor(kb[:, g % 2], bank(B_K),
                                        kmax_all[:].rearrange("c (r d) -> c r d", r=R).unsqueeze(2)
                                        .to_broadcast([P, R, NH, HD]), ALU.subtract).then_inc(ksub_done, 1)

            def keys_inverse(g):
                dve.wait_ge(ctx_ps, g + 1)
                nc.vector.reciprocal(kinv[:, g % 2:g % 2 + 1], ps[:, B_CTX, E:E + 1]).then_inc(kinv_ready, 1)

            def queries_sum(g):
                dve.wait_ge(eq_ready, g + 1)
                nc.vector.tensor_reduce(qsum[:, g % 2], eq[:, g % 2], AX.X, ALU.add).then_inc(qsum_ready, 1)

            def queries_inverse(g):
                dve.wait_ge(qsum_ready, g + 1)
                nc.vector.reciprocal(qinv[:, g % 2], qsum[:, g % 2]).then_inc(qinv_ready, 1)

            def attended_slots(g, at, bank=B_ATT):
                nc.vector.tensor_tensor(att[:, :, g * HD:(g + 1) * HD].rearrange("a (j r) d -> a j r d", r=R)[:, at],
                                        ps[:, bank, :].rearrange("c (h r d) -> c h r d", h=NH, r=R)[:, at],
                                        qinv[:, g % 2, at].unsqueeze(2).unsqueeze(3)
                                        .to_broadcast([P, at.stop - at.start, R, HD]), ALU.mult).then_inc(att_ready, 1)

            def attended(g):
                dve.wait_ge(att_ps, g + 1)
                dve.wait_ge(qinv_ready, g + 1)
                if g < NH - 1:
                    attended_slots(g, slice(0, NH))
                else:
                    attended_slots(g, slice(0, 2), B_Q)

            def attended_rest():
                dve.wait_ge(att_ps, NH + 1)
                attended_slots(NH - 1, slice(2, NH), B_EMB)

            dve.wait_ge(posb_ready, 1)
            for s in STEPS:
                at_block(queries_max, s)
                at_block(keys_max_of_h, s)
                at_block(queries_minus_max, s)
                at_block(keys_max, s)
                at_block(keys_inverse, s - 1)
                at_block(keys_diagonal, s)
                at_block(embed, s + 2)
                at_block(sum1, s + 2)
                at_block(keys_minus_max, s)
                at_block(mean1, s + 2)
                at_block(queries_sum, s)
                at_block(attended, s - 1)
                at_block(squares_sum, s + 2)
                at_block(queries_inverse, s)
                at_block(variance, s + 2)
                if s == -2:
                    dve.wait_ge(bias_rounded, 2)
                    nc.vector.scalar_tensor_tensor(out=bias_rows[:], in0=bias_round[:].bitcast(F32),
                                                   scalar=bias_coef[:, 1:2], in1=bias_part[:],
                                                   op0=ALU.mult, op1=ALU.add).then_inc(biasr_ready, 1)
                if s == 6:
                    dve.wait_ge(rounded, 5)
                    nc.vector.tensor_copy(b2_aug[:, 0:E], b2_round[:, 0:E].bitcast(F32)).then_inc(ffn_w_ready, 1)
                    nc.vector.tensor_tensor(b2_aug[:, E:2 * E], b2_raw[:, E:2 * E], b2_round[:, E:2 * E].bitcast(F32),
                                            ALU.subtract).then_inc(ffn_w_ready, 1)
                    nc.vector.tensor_tensor(wg_hl[:, NX:2 * NX], wg_raw[:], wg_hl[:, 0:NX].bitcast(F32), ALU.subtract)\
                        .then_inc(ffn_w_ready, 1)

            keys_max_of_h(LAST)
            queries_max(LAST)
            keys_max(LAST)
            keys_diagonal(LAST)
            queries_minus_max(LAST)
            keys_minus_max(LAST)
            keys_inverse(LAST - 1)
            queries_sum(LAST)
            queries_inverse(LAST)
            keys_inverse(LAST)
            attended(LAST - 1)
            attended(LAST)

            def slab(u):
                return h2[:].rearrange("a j r e -> a (j r) e")[:, bass.ds(u * GT, GT), :]

            def centre(u, p):
                chain.link(nc.vector.tensor_tensor(slab(u), slab(u), att[:, bass.ds(u * GT, GT), :], ALU.add))
                dve.nop(nofuse=True)
                chain.link(nc.vector.tensor_reduce(s1b[:, p], slab(u), AX.X, ALU.add))
                nc.vector.scalar_tensor_tensor(out=xc2[:, p], in0=s1b[:, p].unsqueeze(2).to_broadcast([P, GT, E]),
                                               scalar=-1.0 / E, in1=slab(u), op0=ALU.mult, op1=ALU.add)\
                    .then_inc(xc2_ready, 1)

            def variance2(u, p):
                dve.wait_ge(sq2_ready, u + 1)
                chain.link(nc.vector.tensor_reduce(s2b[:, p], sq2[:, p], AX.X, ALU.add))
                nc.vector.tensor_scalar(var2[:, p], s2b[:, p], 1.0 / E, EPS, ALU.mult, ALU.add)\
                    .then_inc(var2_ready, 1)

            def split_tokens(u, p):
                for odd in range(2):
                    dve.wait_ge(xh_ready, 2 * u + odd + 1)
                    nc.vector.tensor_tensor(tiles(xhl[p][E:P], odd), tiles_ps(odd),
                                            tiles(xhl[p][0:E], odd).bitcast(F32), ALU.subtract).then_inc(xhl_ready, 1)

            def spread(t):
                return t.unsqueeze(2).to_broadcast([P, GT, NX])

            def top_one(scores, b, n):
                chain.link(nc.vector.tensor_reduce(best[:, 2 * n], scores[:], AX.X, ALU.max))
                chain.link(nc.vector.tensor_tensor(hit[:], scores[:], spread(best[:, 2 * n]), ALU.is_equal))
                chain.link(nc.vector.tensor_tensor(hit[:], hit[:], prio[:].unsqueeze(1).to_broadcast([P, GT, NX]),
                                                   ALU.mult))
                chain.link(nc.vector.tensor_reduce(best[:, 2 * n + 1], hit[:], AX.X, ALU.max))
                chain.link(nc.vector.tensor_tensor(pick[:, n], hit[:], spread(best[:, 2 * n + 1]), ALU.is_equal))

            def route(u, p):
                dve.wait_ge(gate_ps, u + 1)
                gates = ps[:, B_GATE, 0:GT * 2 * NX].rearrange("c (t w x) -> c t w x", t=GT, w=2)
                chain.link(nc.vector.tensor_tensor(score[:], gates[:, :, 0], bg_sb[:].unsqueeze(1)
                                                   .to_broadcast([P, GT, NX]), ALU.add))
                chain.link(nc.vector.tensor_tensor(score[:], gates[:, :, 1], score[:], ALU.add))
                top_one(score, p, 0)
                chain.link(nc.vector.scalar_tensor_tensor(out=score2[:], in0=pick[:, 0], scalar=FAR, in1=score[:],
                                                          op0=ALU.mult, op1=ALU.add))
                top_one(score2, p, 1)
                chain.link(nc.vector.tensor_tensor(mask[:, p, :, NX:2 * NX], pick[:, 0], pick[:, 1], ALU.add))
                nc.vector.tensor_scalar(mask[:, p, :, 0:NX], mask[:, p, :, NX:2 * NX], -1.0, 1.0, ALU.mult, ALU.add)\
                    .then_inc(mask_ready, 1)

            def experts_copy(u, p):
                dve.wait_ge(down_ps, 4 * u + 4)
                nc.vector.tensor_copy(ys[:, p], ps[:, B_DOWN, :]).then_inc(ys_ready, 1)

            def result(u, p):
                dve.wait_ge(yt_ps, u + 1)
                yt = ps[:, B_YT, :].rearrange("c (t y) -> c t y", t=GT)
                chain.link(nc.vector.tensor_tensor(osum[:], yt[:, :, 0:E], slab(u), ALU.add))
                nc.vector.tensor_tensor(o_sb[:, u, :].rearrange("a (r e) -> a r e", r=GT), yt[:, :, E:2 * E],
                                        osum[:], ALU.add).then_inc(out_ready, 1)

            def group(u, p, done=True, prep=True, norm=True, split=True):
                if prep and split:
                    dve.wait_ge(up_ps, 4 * u)
                    split_tokens(u + 1, 1 - p)
                if done:
                    experts_copy(u - 1, 1 - p)
                if prep:
                    route(u + 1, 1 - p)
                if norm:
                    centre(u + 3, 1 - p)
                if done:
                    result(u - 1, 1 - p)
                if norm:
                    variance2(u + 3, 1 - p)

            dve.wait_ge(res_in, 16)
            dve.wait_ge(att_ready, NH)
            centre(0, 0)
            variance2(0, 0)
            attended_rest()
            centre(1, 1)
            variance2(1, 1)
            split_tokens(0, 0)
            route(0, 0)
            split_tokens(1, 1)
            dve.wait_ge(att_ready, NH + 1)
            centre(2, 0)
            variance2(2, 0)
            group(0, 0, done=False, split=False)
            base, before = chain.value, chain.links
            with dve.Fori(0, 6) as i:
                chain.value = base + i * (2 * 18)
                group(2 * i + 1, 1)
                group(2 * i + 2, 0)
                assert chain.links - before == 2 * 18
            chain.value = base + 12 * 18
            group(13, 1, norm=False)
            group(14, 0, norm=False)
            group(15, 1, prep=False, norm=False)
            experts_copy(15, 1)
            result(15, 1)

        @block.tensor
        def _(pe):
            def keep_clock(n, bank):
                for _ in range(n):
                    nc.tensor.transpose(ps[:, bank, 384:512], ident[:], ident[:])

            pe.wait_ge(ld_ident, 16)
            keep_clock(20, 7)
            pe.wait_ge(ld_w, 16 * 4)
            for n in range(4):
                mm = nc.tensor.transpose(ps[:, 7, n * E:(n + 1) * E],
                                         w_rows[:, n].rearrange("o a e -> o (a e)"), ident[0:E, 0:E])
            mm.then_inc(wt_ps, 1)
            for t in range(8):
                if t == 0:
                    keep_clock(8, 0)
                if t % 4 == 0:
                    pe.wait_ge(x_ready[t // 4], 4)
                if t == 7:
                    pe.wait_ge(wbd_ready, 2)
                for f in range(4):
                    mm = nc.tensor.transpose(ps[:, t, f * P:(f + 1) * P],
                                             x_pt[:, 4 * t + f].rearrange("m q p w -> m (q p w)"), ident[:])
                mm.then_inc(pt_ps, 1)
            pe.wait_ge(pt_act, 4)
            pe.wait_ge(pt_dve, 4)

            def embed(g):
                if g:
                    pe.wait_ge(h_ready, g)
                    if g >= 2:
                        pe.wait_ge(xnt_ready, g - 1)
                for b in range(4):
                    mm = nc.tensor.matmul(ps[:, B_EMB, :].rearrange("c (q b e) -> c b q e", q=2, b=4)[:, b],
                                          pt[:, b, g, :], w_bd[:, 0, :], start=True, stop=True)
                mm.then_inc(emb_ps, 1)

            def transpose_tokens(g):
                pe.wait_ge(xn_ready, g + 1)
                pe.wait_ge(h_ready, min(g + 2, NH))
                if g:
                    pe.wait_ge(xnt_ready, g)
                for b in range(4):
                    mm = nc.tensor.transpose(ps[:, B_EMB, b * P:(b + 1) * P], xn[:, g, b * P:(b + 1) * P], ident[:])
                mm.then_inc(xnt_ps, 1)

            def project(g, bank, n, done, bias=True):
                if bias:
                    nc.tensor.matmul(ps[:, bank, :], bias_sel[:],
                                     bias_rows[:, n - 1, :].unsqueeze(1).to_broadcast([P, R, E]),
                                     start=True, stop=False, skip_group_check=True)
                for b in range(4):
                    mm = nc.tensor.matmul(ps[:, bank, b * P:(b + 1) * P], xnt[:, g, b, :], w_bd[:, n, :],
                                          start=not bias, stop=(not bias or b == 3), skip_group_check=True)
                mm.then_inc(done, 1)

            def project_queries(g):
                pe.wait_ge(xnt_ready, g + 1)
                if g:
                    pe.wait_ge(qsub_done, g)
                project(g, B_Q, 1, q_ps)

            def project_keys(g):
                pe.wait_ge(xnt_ready, g + 1)
                if g:
                    pe.wait_ge(ksub_done, g)
                project(g, B_K, 2, k_ps)

            def project_values(g):
                if g:
                    pe.wait_ge(vb_ready, g)
                project(g, B_V, 3, v_ps, bias=False)

            def keys_max(g):
                pe.wait_ge(kmaxh_ready, g + 1)
                if g:
                    pe.wait_ge(kmaxb_ready, g)
                nc.tensor.transpose(ps[0:E, B_KMAX, 0:P], kmax_h[:, g % 2], ident[:]).then_inc(kmaxt_ps, 1)

            def keys_max_spread(g):
                pe.wait_ge(kdiag_ready, g + 1)
                nc.tensor.matmul(ps[:, B_KMAX, P:P + E], ones_row[:], kdiag[:], start=True, stop=True)\
                    .then_inc(kmaxb_ps, 1)

            def transpose_queries(g):
                pe.wait_ge(eq_ready, g + 1)
                if g:
                    pe.wait_ge(eqt_ready, g)
                for n in range(4):
                    mm = nc.tensor.transpose(ps[:, B_EQT, n * P:(n + 1) * P],
                                             eq[:, g % 2, 2 * n:2 * n + 2, :].rearrange("c h f -> c (h f)"), ident[:])
                mm.then_inc(eqt_ps, 1)

            def context(g):
                pe.wait_ge(ek_ready, g + 1)
                pe.wait_ge(vbias_ready, g + 1)
                if g:
                    pe.wait_ge(ctx_ready, 2 * g)
                for h in range(NH):
                    for half in range(2):
                        mm = nc.tensor.matmul(ps[half * E:(half + 1) * E, B_CTX, 0:E + 1], ek[:, g % 2, h, :],
                                              vb[:, g % 2, h, :], start=(h == 0), stop=(h == NH - 1))
                mm.then_inc(ctx_ps, 1)

            def attend(g):
                pe.wait_ge(eqt_ready, g + 1)
                pe.wait_ge(ctx_ready, 2 * (g + 1))
                if g == LAST:
                    pe.wait_ge(qsub_done, NH)
                elif g:
                    pe.wait_ge(att_ready, g)
                for n in range(4):
                    bank = B_ATT if g < LAST else B_EMB if n else B_Q
                    mm = nc.tensor.matmul(ps[:, bank, n * P:(n + 1) * P], eqt[:, g % 2, n, :], ctx_bd[:, g % 2, :],
                                          start=True, stop=True)
                    if n == 3 or (n == 0 and g == LAST):
                        mm.then_inc(att_ps, 1)

            for s in STEPS:
                if s == 0:
                    pe.wait_ge(biasr_ready, 1)
                    pe.wait_ge(zeroed, 10)
                at_block(project_queries, s)
                at_block(project_keys, s)
                at_block(context, s - 1)
                at_block(keys_max, s)
                at_block(embed, s + 2)
                if s == -1:
                    keep_clock(30, B_CTX)
                at_block(project_values, s)
                at_block(keys_max_spread, s)
                at_block(transpose_tokens, s + 1)
                at_block(attend, s - 1)
                at_block(transpose_queries, s)

            project_keys(LAST)
            project_queries(LAST)
            keys_max(LAST)
            project_values(LAST)
            keys_max_spread(LAST)
            context(LAST - 1)
            transpose_queries(LAST)
            context(LAST)
            attend(LAST - 1)
            attend(LAST)

            def transpose2(u, p):
                pe.wait_ge(xn2_ready, u + 1)
                pe.nop(nofuse=True)
                for t in range(2):
                    mm = nc.tensor.transpose(ps[:, B_T, t * P:(t + 1) * P],
                                             xn2[:, p, 2 * t:2 * t + 2, :].rearrange("a t e -> a (t e)"), ident[:])
                mm.then_inc(xt_ps, 1)

            def gate(u, p):
                pe.wait_ge(xhl_ready, 2 * u + 2)
                for t in range(GT):
                    mm = nc.tensor.matmul(ps[:, B_GATE, t * 2 * NX:(t + 1) * 2 * NX], xhl[p][:, t * P:(t + 1) * P],
                                          wg_hl[:], start=True, stop=True)
                mm.then_inc(gate_ps, 1)

            def transpose_mask(u, p):
                pe.wait_ge(mask_ready, u + 1)
                nc.tensor.transpose(ps[:, B_GATE, 0:P], mask[:, p].rearrange("a t m -> a (t m)"), ident[:])\
                    .then_inc(mask_ps, 1)

            def up(u, p, pair, wait_bank=True):
                if wait_bank:
                    pe.wait_ge(hid_ready, 4 * u + pair - 1)
                for k in range(2):
                    e = 2 * pair + k
                    bank = 2 * (pair % 2) + k
                    nc.tensor.matmul(ps[:, bank, :], w1_hh[:, e, :], xhl[p][:], start=True, stop=False)
                    mm = nc.tensor.matmul(ps[:, bank, :], w_aug[:, e * HID:(e + 1) * HID], xm[p][:],
                                          start=False, stop=True)
                mm.then_inc(up_ps, 1)

            def down(u, pair):
                pe.wait_ge(hid_ready, 4 * u + pair + 1)
                for k in range(2):
                    mm = nc.tensor.matmul(ps[k * E:(k + 1) * E, B_DOWN, :], w2_sb[:, 2 * pair + k, :],
                                          hid[:, pair % 2, k, :], start=False, stop=(pair == 3),
                                          skip_group_check=True)
                mm.then_inc(down_ps, 1)

            def down_bias(u, p):
                nc.tensor.matmul(ps[:, B_DOWN, :], b2_aug[:], xm[p][:], start=True, stop=False,
                                 skip_group_check=True)

            def transpose_result(u, p):
                pe.wait_ge(ys_ready, u + 1)
                for t in range(GT):
                    mm = nc.tensor.transpose(ps[:, B_YT, t * P:(t + 1) * P], ys[:, p, t * P:(t + 1) * P], ident[:])
                mm.then_inc(yt_ps, 1)

            def group(u, p, first=False, prep=True):
                if prep and not first:
                    pe.wait_ge(xhl_ready, 2 * u + 2)
                    transpose2(u + 1, 1 - p)
                pe.wait_ge(xmx_ready, u + 1)
                pe.wait_ge(xmm_ready, u + 1)
                up(u, p, 0, not first)
                if not first:
                    down(u - 1, 3)
                if prep:
                    gate(u + 1, 1 - p)
                up(u, p, 1, not first)
                if not first:
                    pe.wait_ge(ys_ready, u)
                down_bias(u, p)
                down(u, 0)
                up(u, p, 2)
                down(u, 1)
                if not first:
                    transpose_result(u - 1, 1 - p)
                if prep:
                    transpose_mask(u + 1, 1 - p)
                up(u, p, 3)
                down(u, 2)

            keep_clock(35, B_CTX)
            pe.wait_ge(att_ready, NH + 1)
            pe.wait_ge(ffn_w_ready, 4)
            transpose2(0, 0)
            keep_clock(5, B_YT)
            gate(0, 0)
            transpose2(1, 1)
            keep_clock(26, B_YT)
            transpose_mask(0, 0)
            group(0, 0, first=True)
            with pe.Fori(0, 6) as i:
                group(2 * i + 1, 1)
                group(2 * i + 2, 0)
            group(13, 1)
            group(14, 0)
            group(15, 1, prep=False)
            down(15, 3)
            transpose_result(15, 1)


_INS = ['x', 'L0_tok_W', 'L0_tok_b', 'L0_tok_pos_embed', 'L0_attn_Wq', 'L0_attn_bq', 'L0_attn_Wk', 'L0_attn_bk',
        'L0_attn_Wv', 'L0_attn_bv', 'L0_ffn_Wg', 'L0_ffn_bg', 'L0_ffn_W1', 'L0_ffn_b1', 'L0_ffn_W2', 'L0_ffn_b2']


def _constants(np):
    rows = np.zeros((16, NX, HID), np.float32)
    for e in range(NX):
        rows[e, e, :] = -BIG
    coef = np.zeros((KM, 2), np.float32)
    coef[0:E] = (1.0, -1.0)
    coef[E:E + 16] = (1.0, 0.0)
    coef[E + 16] = (0.0, 1.0)
    coef[E + 17] = (1.0, -1.0)
    prio = np.tile(np.arange(NX, 0, -1, dtype=np.float32), (P, 1))
    bias = np.zeros((P, 2), np.float32)
    bias[0] = (0.0, 1.0)
    bias[1] = (1.0, -1.0)
    return {"ident": np.eye(P, dtype=np.float32), "rows": rows.reshape(16, NX * HID), "coef": coef,
            "prio": prio, "bias": bias}


def kernel(**inputs):
    import numpy as _np
    import concourse.bacc as _bacc
    from concourse import mybir as _mybir
    from concourse.bass_utils import run_bass_kernel_spmd as _run

    nc = _bacc.Bacc("TRN2", target_bir_lowering=False, num_devices=1)
    arrays, args = {}, []
    for name in _INS:
        a = _np.ascontiguousarray(inputs[name])
        arrays[f"in_{name}_dram"] = a
        args.append(nc.dram_tensor(f"in_{name}_dram", a.shape, _mybir.dt.from_np(a.dtype), kind="ExternalInput").ap())
    for name, a in _constants(_np).items():
        arrays[f"const_{name}_dram"] = a
        args.append(nc.dram_tensor(f"const_{name}_dram", a.shape, _mybir.dt.from_np(a.dtype), kind="ExternalInput").ap())
    args.append(nc.dram_tensor("out_0_dram", (R, C, E), _mybir.dt.float32, kind="ExternalOutput").ap())
    bass_vit_layer_kernel(nc, *args)
    r = _run(nc, [arrays], core_ids=[0])
    return r.results[0]["out_0_dram"]
```
